# Optimizing a Trainium2 kernel written in Bass

```python
import numpy as np
import jax
import jax.numpy as jnp

def _softmax(x, axis=-1):
    return jax.nn.softmax(x, axis=axis)

def _gelu(x):
    return jax.nn.gelu(x, approximate=True)

def _silu(x):
    return jax.nn.silu(x)

def _sigmoid(x):
    return jax.nn.sigmoid(x)

def _layernorm(x, axis=-1, eps=1e-05):
    m = jnp.mean(x, axis=axis, keepdims=True)
    v = jnp.var(x, axis=axis, keepdims=True)
    return (x - m) / jnp.sqrt(v + eps)

def _scatter_add(tgt, idx, src, axis=0):
    return tgt.at[idx].add(src)

def _segment_sum(src, seg, n):
    return jax.ops.segment_sum(src, seg, n)
kernel_name = 'mk_gnn_resnorm_d1_gnn_r8_9aa351'

def setup_inputs(seed: int=0):
    np.random.seed(seed)
    _w = jnp.asarray

    def _rec_inputs():
        import jax
        import jax.numpy as jnp
        _gk = jax.random.key(seed)
        x = -0.0003929 + 0.9999 * jax.random.normal(jax.random.fold_in(_gk, 1), (4096, 512), jnp.float32)
        src = jax.random.randint(jax.random.fold_in(_gk, 2), (131072,), 0, 4096, jnp.int32)
        dst = jnp.minimum((4096 * jax.random.uniform(jax.random.fold_in(_gk, 3), (131072,)) ** 2.0).astype(jnp.int32), 32767)
        _o = jnp.argsort(dst, stable=True)
        src = src[_o]
        dst = dst[_o]
        edge_attr_8 = -4.48278e-06 + 1.00019 * jax.random.normal(jax.random.fold_in(_gk, 12), (131072, 8), jnp.float32)
        return (x, src, dst, edge_attr_8)
    x, src, dst, edge_attr_8 = _rec_inputs()

    def _L0_gnn_setup():
        import jax, jax.numpy as jnp
        import numpy as np
        L, C, H, E = (4096, 512, 8, 131072)
        D = C // H
        HID = 1024
        EPS = 1e-05

        def _ln(x, g, b):
            mu = jnp.mean(x, axis=-1, keepdims=True)
            var = jnp.var(x, axis=-1, keepdims=True)
            return (x - mu) * jax.lax.rsqrt(var + EPS) * g + b

        def _sparse_attention(z, row, col, bias, Wq, bq, Wk, bk, Wv, bv, Wo, bo):
            q = (z @ Wq + bq).reshape(L, H, D)
            k = (z @ Wk + bk).reshape(L, H, D)
            v = (z @ Wv + bv).reshape(L, H, D)
            scale = 1.0 / jnp.sqrt(jnp.asarray(D, z.dtype))
            scores = jnp.einsum('ehd,ehd->eh', q[row], k[col]) * scale + bias
            m = jax.ops.segment_max(scores, row, num_segments=L)
            p = jnp.exp(scores - m[row])
            ssum = jax.ops.segment_sum(p, row, num_segments=L)
            alpha = p / ssum[row]
            out = jax.ops.segment_sum(alpha[:, :, None] * v[col], row, num_segments=L)
            return out.reshape(L, C) @ Wo + bo
        key = jax.random.key(seed)
        ks = jax.random.split(key, 12)
        s = 0.02
        inp = {'x': jax.random.normal(ks[0], (L, C), jnp.float32), 'row_index': jnp.sort(jax.random.randint(ks[1], (E,), 0, L)), 'col_index': jax.random.randint(ks[2], (E,), 0, L), 'att_bias': jax.random.normal(ks[3], (E, H), jnp.float32), 'Wq': jax.random.normal(ks[4], (C, C), jnp.float32) * s, 'bq': jnp.zeros((C,), jnp.float32), 'Wk': jax.random.normal(ks[5], (C, C), jnp.float32) * s, 'bk': jnp.zeros((C,), jnp.float32), 'Wv': jax.random.normal(ks[6], (C, C), jnp.float32) * s, 'bv': jnp.zeros((C,), jnp.float32), 'Wo': jax.random.normal(ks[7], (C, C), jnp.float32) * s, 'bo': jnp.zeros((C,), jnp.float32), 'ln1_g': jnp.ones((C,), jnp.float32), 'ln1_b': jnp.zeros((C,), jnp.float32), 'ln2_g': jnp.ones((C,), jnp.float32), 'ln2_b': jnp.zeros((C,), jnp.float32), 'W1': jax.random.normal(ks[8], (C, HID), jnp.float32) * s, 'b1': jnp.zeros((HID,), jnp.float32), 'W2': jax.random.normal(ks[9], (HID, C), jnp.float32) * s, 'b2': jnp.zeros((C,), jnp.float32)}
        return inp
    _L0_gnn_all = _L0_gnn_setup()
    _L0_gnn_in = {k: v for k, v in _L0_gnn_all.items() if k in ('Wq', 'bq', 'Wk', 'bk', 'Wv', 'bv', 'Wo', 'bo', 'ln1_g', 'ln1_b', 'ln2_g', 'ln2_b', 'W1', 'b1', 'W2', 'b2')}
    del _L0_gnn_all
    return {'x': x, 'src': src, 'dst': dst, 'edge_attr_8': edge_attr_8, 'L0_gnn_Wq': _L0_gnn_in['Wq'], 'L0_gnn_bq': _L0_gnn_in['bq'], 'L0_gnn_Wk': _L0_gnn_in['Wk'], 'L0_gnn_bk': _L0_gnn_in['bk'], 'L0_gnn_Wv': _L0_gnn_in['Wv'], 'L0_gnn_bv': _L0_gnn_in['bv'], 'L0_gnn_Wo': _L0_gnn_in['Wo'], 'L0_gnn_bo': _L0_gnn_in['bo'], 'L0_gnn_ln1_g': _L0_gnn_in['ln1_g'], 'L0_gnn_ln1_b': _L0_gnn_in['ln1_b'], 'L0_gnn_ln2_g': _L0_gnn_in['ln2_g'], 'L0_gnn_ln2_b': _L0_gnn_in['ln2_b'], 'L0_gnn_W1': _L0_gnn_in['W1'], 'L0_gnn_b1': _L0_gnn_in['b1'], 'L0_gnn_W2': _L0_gnn_in['W2'], 'L0_gnn_b2': _L0_gnn_in['b2']}

def reference(x, src, dst, edge_attr_8, L0_gnn_Wq, L0_gnn_bq, L0_gnn_Wk, L0_gnn_bk, L0_gnn_Wv, L0_gnn_bv, L0_gnn_Wo, L0_gnn_bo, L0_gnn_ln1_g, L0_gnn_ln1_b, L0_gnn_ln2_g, L0_gnn_ln2_b, L0_gnn_W1, L0_gnn_b1, L0_gnn_W2, L0_gnn_b2):
    import jax
    import jax.numpy as jnp

    def _L0_gnn_ref(x, att_bias, Wq, bq, Wk, bk, Wv, bv, Wo, bo, ln1_g, ln1_b, ln2_g, ln2_b, W1, b1, W2, b2, row_index, col_index):
        import jax, jax.numpy as jnp
        import numpy as np
        L, C, H, E = (4096, 512, 8, 131072)
        D = C // H
        HID = 1024
        EPS = 1e-05

        def _ln(x, g, b):
            mu = jnp.mean(x, axis=-1, keepdims=True)
            var = jnp.var(x, axis=-1, keepdims=True)
            return (x - mu) * jax.lax.rsqrt(var + EPS) * g + b

        def _sparse_attention(z, row, col, bias, Wq, bq, Wk, bk, Wv, bv, Wo, bo):
            q = (z @ Wq + bq).reshape(L, H, D)
            k = (z @ Wk + bk).reshape(L, H, D)
            v = (z @ Wv + bv).reshape(L, H, D)
            scale = 1.0 / jnp.sqrt(jnp.asarray(D, z.dtype))
            scores = jnp.einsum('ehd,ehd->eh', q[row], k[col]) * scale + bias
            m = jax.ops.segment_max(scores, row, num_segments=L)
            p = jnp.exp(scores - m[row])
            ssum = jax.ops.segment_sum(p, row, num_segments=L)
            alpha = p / ssum[row]
            out = jax.ops.segment_sum(alpha[:, :, None] * v[col], row, num_segments=L)
            return out.reshape(L, C) @ Wo + bo
        z = _ln(x, ln1_g, ln1_b)
        att = _sparse_attention(z, row_index, col_index, att_bias, Wq, bq, Wk, bk, Wv, bv, Wo, bo)
        x = x + att
        z = _ln(x, ln2_g, ln2_b)
        ff = jax.nn.silu(z @ W1 + b1) @ W2 + b2
        return x + ff
    x = _layernorm(x + _L0_gnn_ref(x, edge_attr_8, L0_gnn_Wq, L0_gnn_bq, L0_gnn_Wk, L0_gnn_bk, L0_gnn_Wv, L0_gnn_bv, L0_gnn_Wo, L0_gnn_bo, L0_gnn_ln1_g, L0_gnn_ln1_b, L0_gnn_ln2_g, L0_gnn_ln2_b, L0_gnn_W1, L0_gnn_b1, L0_gnn_W2, L0_gnn_b2, src, dst), axis=-1)
    return x

_drawn_inputs = setup_inputs


def setup_inputs(seed=0):
    import zlib

    import numpy as np

    out = dict(_drawn_inputs(seed))
    spreads = {'L0_gnn_bq': (0.0, 0.8),
     'L0_gnn_bk': (0.0, 2.0),
     'L0_gnn_bv': (0.0, 0.342),
     'L0_gnn_bo': (0.0, 0.1),
     'L0_gnn_ln1_g': (1.0, 0.6),
     'L0_gnn_ln1_b': (0.0, 0.8),
     'L0_gnn_ln2_g': (1.0, 0.6),
     'L0_gnn_ln2_b': (0.0, 0.8),
     'L0_gnn_b1': (0.0, 0.461),
     'L0_gnn_b2': (0.0, 0.1)}
    factors = {'L0_gnn_Wq': 8.0, 'L0_gnn_Wk': 8.0, 'edge_attr_8': 2.866}
    for name, (base, spread) in spreads.items():
        noise = np.random.default_rng([zlib.crc32(name.encode()), seed]).standard_normal(out[name].shape)
        drawn = base * np.exp(spread * noise) if base else spread * noise
        out[name] = jnp.asarray(drawn.astype(out[name].dtype))
    for name, factor in factors.items():
        out[name] = (out[name] * factor).astype(out[name].dtype)
    return out
```

```python
from contextlib import ExitStack

import concourse.bass as bass
from concourse import mybir

F32 = mybir.dt.float32
BF16 = mybir.dt.bfloat16
I32 = mybir.dt.int32
ALU = mybir.AluOpType
ACT = mybir.ActivationFunctionType
AX = mybir.AxisListType

P = 128
HEADS = 8
GROUP = 8
SUB = GROUP // 2
STREAMS = 8
REC = 12
LO = 64
EPS = 1e-5
PAD_BIAS = -3.0e38
FLOOR = -1.0e38
TINY = 1.0e-30
RESET_AT = 400
NO_COL = 1 << 20


def layer_kernel(nc, x, src, dst, edge_bias, Wq, bq, Wk, bk, Wv, bv, Wo, bo, ln1_g, ln1_b,
                 ln2_g, ln2_b, W1, b1, W2, b2, out):
    L, C = x.shape
    E = src.shape[0]
    HID = W1.shape[1]
    D = C // HEADS
    NT = L // P
    KT = C // P
    HT = HID // P
    HI = L // LO
    COLS = E // P
    STEPS = COLS // STREAMS
    SPI = STEPS // NT
    TB = COLS // P
    RPP = L // P
    NBLK = E // GROUP + 2 * L
    PADN = 96
    SCALE = float(D) ** -0.5
    assert SPI % 2 == 0 and SPI * NT == STEPS and (NBLK * GROUP) % (P * PADN) == 0

    srcT = nc.dram_tensor("srcT", [COLS, P], F32, kind="Internal").ap()
    hiT = nc.dram_tensor("hiT", [COLS, P], F32, kind="Internal").ap()
    records = nc.dram_tensor("records", [NBLK * GROUP, REC], F32, kind="Internal").ap()
    row_info = nc.dram_tensor("row_info", [L, 4], F32, kind="Internal").ap()
    row_key = nc.dram_tensor("row_key", [L], F32, kind="Internal").ap()
    rows_ranked = nc.dram_tensor("rows_ranked", [L, 4], F32, kind="Internal").ap()
    n_groups = nc.dram_tensor("n_groups", [1, NT], I32, kind="Internal").ap()
    qx = nc.dram_tensor("qx", [L, 2 * C], F32, kind="Internal").ap()
    kv = nc.dram_tensor("kv", [L, 2 * C], F32, kind="Internal").ap()
    blocks = records.rearrange("(n g) r -> n (g r)", g=GROUP)

    with ExitStack() as ctx:
        def sb(name, shape, dt=F32):
            return ctx.enter_context(nc.sbuf_tensor(name, shape, dt))

        def sem(name):
            return ctx.enter_context(nc.semaphore(name))

        region_a = sb("region_a", [P, 2 * GROUP * 2 * C])
        KV = [region_a[:, h * GROUP * 2 * C:(h + 1) * GROUP * 2 * C].rearrange("p (s c) -> p s c", s=GROUP)
              for h in range(2)]
        edge_sb = region_a[:, 0:COLS * HEADS]
        at = COLS * HEADS
        src_f, hi_f, lo_f = (region_a[:, at + i * COLS:at + (i + 1) * COLS] for i in range(3))
        int_a, int_b, dst_i = (region_a[:, at + i * COLS:at + (i + 1) * COLS].bitcast(I32) for i in range(3, 6))
        region_b = sb("region_b", [P, KT * C + KT * HID + HT * C])
        Wqkv = region_b[:, 0:3 * KT * C].rearrange("p (w k n) -> p w k n", w=3, k=KT)
        keys_all = region_b[:, 3 * KT * C:3 * KT * C + L]
        Wo_sb = region_b[:, 0:KT * C].rearrange("p (k n) -> p k n", k=KT)
        W1_sb = region_b[:, KT * C:KT * C + KT * HID].rearrange("p (k n) -> p k n", k=KT)
        W2_sb = region_b[:, KT * C + KT * HID:].rearrange("p (k n) -> p k n", k=HT)
        region_c = sb("region_c", [P, 12800])
        pos_c = [0]

        def part(words):
            v = region_c[:, pos_c[0]:pos_c[0] + words]
            pos_c[0] += words
            return v

        srcb = [part(STREAMS * P) for _ in range(2)]
        hib = [part(STREAMS * P)[0:HI, :] for _ in range(2)]
        hitT = [part(STREAMS * P)[0:HI, :] for _ in range(2)]
        sel = part(STREAMS * LO)
        eq = part(STREAMS * P // 2).bitcast(BF16)
        table_sb = part(STREAMS * LO)[0:HI, :]
        qx_row, kv_row = part(2 * C), part(2 * C)
        z1, zT1 = part(C), part(C)
        greater = part(L // 2).bitcast(BF16)
        used_sort = pos_c[0]
        pos_c[0] = 0
        q_w, x_w, stage = part(C), part(C), part(2 * C)
        acc, att, attT = part(C), part(C), part(C)
        s_w, z2, z2T, out_w = part(C), part(C), part(C), part(C)
        th, hb, hT = part(HID), part(HID), part(HID)
        prods = part(GROUP * C).rearrange("p (s c) -> p s c", s=GROUP)
        assert max(used_sort, pos_c[0]) <= 12800

        pad_rec = sb("pad_rec", [P, PADN, REC])
        rec_w = [sb(f"rec_w{i}", [P, STREAMS, REC]) for i in range(2)]
        hi_oh = [sb(f"hi_oh{i}", [P, STREAMS, HI], BF16) for i in range(2)]
        lo_oh = [sb(f"lo_oh{i}", [P, STREAMS, LO], BF16) for i in range(2)]
        rank_w = sb("rank_w", [P, STREAMS])
        base_w = sb("base_w", [P, STREAMS])
        pos_i = [sb(f"pos_i{i}", [P, STREAMS], I32) for i in range(2)]
        iota_i = sb("iota_i", [P, P], I32)
        iota_f = sb("iota_f", [P, P])
        part_i = sb("part_i", [P, 1], I32)
        part_f = sb("part_f", [P, 1])
        ident = sb("ident", [P, P])
        tri = sb("tri", [P, P])
        triT = sb("triT", [P, P])
        ones = sb("ones", [1, P])
        zeros_bf = sb("zeros_bf", [P, STREAMS * LO], BF16)
        eps_t = sb("eps_t", [P, 1])
        hist = sb("hist", [HI, STREAMS, LO])
        start_tab = sb("start_tab", [HI, STREAMS, LO])
        deg = sb("deg", [HI, LO])
        deg_i = sb("deg_i", [HI, LO], I32)
        nb_i = sb("nb_i", [HI, LO], I32)
        width = sb("width", [HI, LO])
        cum = sb("cum", [HI, LO])
        blk = sb("blk", [HI, LO])
        ones_lo = sb("ones_lo", [HI, LO])
        rid_i = sb("rid_i", [HI, LO], I32)
        rid_f = sb("rid_f", [HI, LO])
        key_w = sb("key_w", [HI, LO])
        info_w = sb("info_w", [HI, LO, 4])
        offs = sb("offs", [HI, 1])
        key_col = sb("key_col", [P, RPP])
        rank_f = sb("rank_f", [P, RPP])
        rank_i = sb("rank_i", [P, RPP], I32)
        info_sb = sb("info_sb", [P, RPP, 4])
        ranked_sb = sb("ranked_sb", [NT, P, 4])
        ng_f = sb("ng_f", [NT, 1])
        ng_i = sb("ng_i", [NT, 1], I32)
        bias3 = sb("bias3", [1, 3 * C])
        bias2 = sb("bias2", [1, 2 * C])
        ln1_cols = sb("ln1_cols", [P, 2, KT])
        ln2_cols = sb("ln2_cols", [P, 2, KT])
        b1_col = sb("b1_col", [P, HT])
        b1_half = sb("b1_half", [P, HT])
        stats = sb("stats", [P, 6])
        mv = sb("mv", [P, 2])
        std = sb("std", [P, 1])
        rstd = sb("rstd", [P, 1])
        perm = sb("perm", [P, NT + 1])
        row_w = sb("row_w", [P, 4])
        idx = [sb(f"idx{i}", [P, 1], I32) for i in range(2)]
        out_idx = sb("out_idx", [P, 1], I32)
        rec = [sb(f"rec{i}", [P, GROUP, REC]) for i in range(2)]
        sc = [sb(f"sc{i}", [P, GROUP + 1, HEADS]) for i in range(2)]
        pr = [sb(f"pr{i}", [P, GROUP + 1, HEADS]) for i in range(2)]
        m_run = sb("m_run", [P, HEADS])
        m_new = sb("m_new", [P, HEADS])
        l_run = sb("l_run", [P, HEADS])
        l_sum = sb("l_sum", [P, HEADS])
        l_inv = sb("l_inv", [P, HEADS])

        bank = [ctx.enter_context(nc.psum_tensor(f"bank{i}", [P, 512], F32)) for i in range(8)]
        count_ps = bank[0][0:HI, :]
        sel_ps = bank[1]
        turn_ps = bank[2]
        qkv_ps = bank[3:6]
        pv_ps = bank[0:2]
        wo_ps, y_ps = bank[3], bank[4]
        h_ps = bank[5:7]

        names = """kv00 kv01 kv10 kv11 rec_loaded src_loaded edges_loaded weights_loaded consts_a pad_ready
            table_cleared keys_ready turned turned_sb turned_out onehots_free onehots_ready hist_done prefix_in
            prefix_out info_ready info_out keys_loaded srcb0 srcb1 srcb_used hit_ready g_done sel_free oh1_ready
            counted1 table_ready pos_ready rec_ready scat0 scat1 x_loaded stats1 std1 z1_ready z1_turned z1_sb
            qkv_done qkv_sb qkv_out rank_ready ranked ranked_loaded ng_ready ng_out phase1_dve phase1_act
            phase1_pe weights2 row_loaded row_used stage_loaded q_ready x_ready idx_set bias_used0 bias_used1
            sc0 sc1 ex0 ex1 pv00 pv01 pv10 pv11 pe00 pe01 pe10 pe11 pv_free0 pv_free1 att_ready att_turned
            att_sb wo_done z2_ready z2_turned z2_sb h_done h_act h_ready y_done out_ready out_sent consts_c
            q_used s_ready quiet restarted pool_held dve_held stats_end stats_mid std_end std_mid""".split()
        S = {n: sem(n) for n in names}
        SRCB = [S["srcb0"], S["srcb1"]]
        SCAT = [S["scat0"], S["scat1"]]
        DMA_COUNTS = [S[n] for n in ("kv00", "kv01", "kv10", "kv11", "rec_loaded")]
        KVS = [[S["kv00"], S["kv01"]], [S["kv10"], S["kv11"]]]
        PVS = [[S["pv00"], S["pv01"]], [S["pv10"], S["pv11"]]]
        PES = [[S["pe00"], S["pe01"]], [S["pe10"], S["pe11"]]]
        SC, EX = [S["sc0"], S["sc1"]], [S["ex0"], S["ex1"]]
        BIAS_USED = [S["bias_used0"], S["bias_used1"]]
        PV_FREE = [S["pv_free0"], S["pv_free1"]]

        block = ctx.enter_context(nc.Block())

        def load_count(eng, t):
            return eng.value_load(n_groups[0:1, bass.ds(t, 1)], min_val=1, max_val=NBLK)

        def tile_groups(eng, n, half, between=None, after=None, reset=None):
            half(0, first=True)
            if between:
                between()
            with eng.If(n > 1):
                half(1, first=False)
            if after:
                after()
            with eng.If(n > 2):
                with eng.Fori(1, (n + 1) // 2) as i:
                    if reset:
                        reset()
                    half(0, first=False)
                    with eng.If(i * 2 + 1 < n):
                        half(1, first=False)

        @block.sync
        def _(sp):
            sp.dma_start(int_a, src.rearrange("(p c) -> p c", p=P)).then_inc(S["src_loaded"], 16)
            sp.dma_start(dst_i, dst.rearrange("(p c) -> p c", p=P)).then_inc(S["edges_loaded"], 16)
            sp.dma_start(edge_sb, edge_bias.rearrange("(p c) h -> p (c h)", p=P)).then_inc(S["edges_loaded"], 16)
            sp.wait_ge(S["pad_ready"], 3)
            flat = records.rearrange("(n p k) r -> n p (k r)", p=P, k=PADN)
            for n in range(flat.shape[0]):
                sp.dma_start(flat[n], pad_rec[:, :, :].rearrange("p k r -> p (k r)")).then_inc(S["table_cleared"], 16)
            for w, W in enumerate((Wq, Wk, Wv)):
                sp.dma_start(Wqkv[:, w], W.rearrange("(k p) n -> p k n", p=P)).then_inc(S["weights_loaded"], 16)
            for w, b in enumerate((bq, bk, bv)):
                sp.dma_start(bias3[:, w * C:(w + 1) * C], b.rearrange("(a n) -> a n", a=1)).then_inc(S["weights_loaded"], 16)
            for w, b in enumerate((bo, b2)):
                sp.dma_start(bias2[:, w * C:(w + 1) * C], b.rearrange("(a n) -> a n", a=1)).then_inc(S["weights_loaded"], 16)
            with nc.allow_non_contiguous_dma(reason="vectors of a few KB to columns"):
                for to, (g, b) in ((ln1_cols, (ln1_g, ln1_b)), (ln2_cols, (ln2_g, ln2_b))):
                    sp.dma_start(to[:, 0, :], g.rearrange("(k p) -> p k", p=P)).then_inc(S["weights_loaded"], 16)
                    sp.dma_start(to[:, 1, :], b.rearrange("(k p) -> p k", p=P)).then_inc(S["weights_loaded"], 16)
                sp.dma_start(b1_col[:, :], b1.rearrange("(k p) -> p k", p=P)).then_inc(S["weights_loaded"], 16)
            sp.wait_ge(S["turned_sb"], 2)
            for to, of in ((srcT, qx_row), (hiT, kv_row)):
                sp.dma_start(to.rearrange("(b c) e -> c b e", c=P),
                             of[:, 0:COLS].rearrange("p (b e) -> p b e", b=TB)).then_inc(S["turned_out"], 16)
            sp.wait_ge(S["info_ready"], 1)
            sp.dma_start(row_info.rearrange("(h l) w -> h (l w)", h=HI),
                         info_w[:, :, :].rearrange("h l w -> h (l w)")).then_inc(S["info_out"], 16)
            sp.dma_start(row_key.rearrange("(h l) -> h l", h=HI), key_w[:, :]).then_inc(S["info_out"], 16)
            sp.wait_ge(S["info_out"], 32)
            sp.dma_start(info_sb[:, :, :], row_info.rearrange("(p j) w -> p j w", p=P)).then_inc(S["keys_loaded"], 16)
            sp.dma_start(key_col[:, :], row_key.rearrange("(p j) -> p j", p=P)).then_inc(S["keys_loaded"], 16)
            sp.dma_start(keys_all, row_key.rearrange("(a n) -> a n", a=1).broadcast_to([P, L])).then_inc(S["keys_loaded"], 16)
            sp.wait_ge(S["turned_out"], 32)
            chunk = srcT.rearrange("(s c) e -> s (c e)", c=STREAMS)
            chunk_hi = hiT.rearrange("(s c) e -> s (c e)", c=STREAMS)
            with sp.Fori(0, NT) as it:
                sp.wait_ge(S["qkv_out"], it * 32)
                sp.dma_start(qx_row[:, C:2 * C], x[bass.ts(it, P), :]).then_inc(S["x_loaded"], 16)
                for j in range(SPI):
                    sp.wait_ge(S["srcb_used"], it * SPI + j + 1)
                    sp.dma_start(srcb[j % 2], chunk[bass.ds(it * SPI + j, 1), :].broadcast_to([P, STREAMS * P])).then_inc(SRCB[j % 2], 16)
                    sp.dma_start(hib[j % 2], chunk_hi[bass.ds(it * SPI + j, 1), :].broadcast_to([HI, STREAMS * P])).then_inc(SRCB[j % 2], 16)
                sp.wait_ge(S["qkv_sb"], it * 3 + 3)
                sp.dma_start(qx[bass.ts(it, P), :], qx_row).then_inc(S["qkv_out"], 16)
                sp.dma_start(kv[bass.ts(it, P), :], kv_row).then_inc(S["qkv_out"], 16)
            sp.wait_ge(S["phase1_pe"], 1)
            sp.wait_ge(S["phase1_dve"], 1)
            sp.dma_start(Wo_sb, Wo.rearrange("(k p) n -> p k n", p=P)).then_inc(S["weights2"], 16)
            sp.dma_start(W1_sb, W1.rearrange("(k p) n -> p k n", p=P)).then_inc(S["weights2"], 16)
            sp.dma_start(W2_sb, W2.rearrange("(k p) n -> p k n", p=P)).then_inc(S["weights2"], 16)
            sp.wait_ge(S["ranked"], 16 * RPP)
            sp.dma_start(ranked_sb[:, :, :], rows_ranked.rearrange("(t p) w -> t p w", p=P)).then_inc(S["ranked_loaded"], 16)
            with nc.allow_non_contiguous_dma(reason="one word a row"):
                sp.dma_start(perm[:, 1:], rows_ranked[:, 0:1].rearrange("(t p) w -> p (t w)", p=P)).then_inc(S["ranked_loaded"], 16)
                sp.wait_ge(S["ng_ready"], 1)
                sp.dma_start(n_groups.rearrange("a t -> t a"), ng_i[:, :]).then_inc(S["ng_out"], 16)
            with sp.Fori(0, NT) as t:
                sp.wait_ge(S["row_used"], t)
                sp.dma_start(row_w[:, :], rows_ranked[bass.ts(t, P), :]).then_inc(S["row_loaded"], 16)

        @block.gpsimd
        def _(pool):
            def hold(semaphore, value):
                pool.wait_ge(semaphore, value)
                pool.sem_inc(S["pool_held"], 1)

            pool.iota(iota_i[:, :], pattern=[[1, P]], base=0, channel_multiplier=0).then_inc(S["consts_a"], 1)
            pool.iota(part_i[:, :], pattern=[[0, 1]], base=0, channel_multiplier=1).then_inc(S["consts_a"], 1)
            pool.iota(rid_i[:, :], pattern=[[1, LO]], base=0, channel_multiplier=LO).then_inc(S["consts_a"], 1)
            pool.memset(pad_rec[:, :, 0:HEADS], PAD_BIAS).then_inc(S["pad_ready"], 1)
            pool.memset(pad_rec[:, :, HEADS:HEADS + 1].bitcast(I32), NO_COL).then_inc(S["pad_ready"], 1)
            pool.memset(pad_rec[:, :, HEADS + 1:REC], 0.0).then_inc(S["pad_ready"], 1)
            pool.memset(rec_w[0][:, :, HEADS + 1:REC], 0.0).then_inc(S["consts_c"], 1)
            pool.memset(rec_w[1][:, :, HEADS + 1:REC], 0.0).then_inc(S["consts_c"], 1)
            pool.memset(region_a[:, COLS * (HEADS + 6):], 0.0).then_inc(S["consts_c"], 1)
            pool.wait_ge(S["consts_c"], 3)
            pool.wait_ge(S["table_cleared"], 16 * (NBLK * GROUP // (P * PADN)))
            with pool.Fori(0, NT) as it:
                for j in range(SPI):
                    hold(S["pos_ready"], it * SPI + j + 1)
                    hold(S["rec_ready"], it * SPI + j + 1)
                    for s in range(STREAMS):
                        pool.indirect_dma_start(records, bass.IndirectOffsetOnAxis(ap=pos_i[j % 2][:, s:s + 1], axis=0),
                                                rec_w[j % 2][:, s, :], None).then_inc(SCAT[j % 2], 16)
            pool.wait_ge(S["rank_ready"], 1)
            for j in range(RPP):
                pool.indirect_dma_start(rows_ranked, bass.IndirectOffsetOnAxis(ap=rank_i[:, j:j + 1], axis=0),
                                        info_sb[:, j, :], None).then_inc(S["ranked"], 16)
            for h in range(2):
                pool.wait_ge(SCAT[h], 16 * STREAMS * STEPS // 2)
            pool.wait_ge(S["qkv_out"], 32 * NT)
            pool.wait_ge(S["phase1_dve"], 1)
            pool.wait_ge(S["phase1_act"], 1)
            pool.wait_ge(S["ng_out"], 16)
            used = [pool.alloc_register(f"pool_used{h}") for h in range(2)]
            n_rec = pool.alloc_register("pool_recs")
            n_idx = pool.alloc_register("pool_idx")
            n_out = pool.alloc_register("pool_outs")
            since = pool.alloc_register("pool_since")
            n_resets = pool.alloc_register("pool_resets")
            for r in (*used, n_rec, n_idx, n_out, since, n_resets):
                pool.reg_mov(r, 0)

            def load_records(h):
                pool.reg_add(n_rec, n_rec, 1)
                pool.indirect_dma_start(rec[h][:, :, :].rearrange("p s r -> p (s r)"), None, blocks,
                                        bass.IndirectOffsetOnAxis(ap=idx[h][:, 0:1], axis=0)).then_inc(S["rec_loaded"], 16)

            def half(h, first):
                u = pool.snap(used[h])
                k = pool.snap(n_idx)
                hold(S["rec_loaded"], pool.snap(n_rec) * 16)
                for a in range(2):
                    hold(PES[h][a], u)
                    for s in range(a * SUB, (a + 1) * SUB):
                        pool.indirect_dma_start(KV[h][:, s, :], None, kv,
                                                bass.IndirectOffsetOnAxis(ap=rec[h][:, s, HEADS:HEADS + 1].bitcast(I32), axis=0),
                                                bounds_check=L - 1, oob_is_err=False).then_inc(KVS[h][a], 16)
                pool.tensor_scalar(idx[1 - h][:, :], idx[h][:, :], 1.0, row_w[:, 2:3], ALU.add, ALU.min).then_inc(S["idx_set"], 1)
                pool.reg_add(n_idx, n_idx, 1)
                pool.reg_add(used[h], used[h], 1)
                if h == 0:
                    pool.reg_add(since, since, 1)
                hold(S["idx_set"], k + 1)
                hold(BIAS_USED[1 - h], pool.snap(used[1 - h]))
                load_records(1 - h)

            def reset():
                with pool.If(pool.snap(since) > RESET_AT):
                    pool.reg_add(n_resets, n_resets, 1)
                    hold(S["quiet"], pool.snap(n_resets))
                    pool.drain()
                    pool.dma_reset(range(DMA_COUNTS[0].num, DMA_COUNTS[-1].num + 1))
                    pool.sem_clear(range(DMA_COUNTS[0].num, DMA_COUNTS[-1].num + 1))
                    pool.reg_mov(n_rec, 0)
                    pool.reg_mov(since, 0)
                    pool.drain().then_inc(S["restarted"], 1)

            with pool.Fori(0, NT) as t:
                n = load_count(pool, t)
                hold(S["row_loaded"], t * 16 + 16)
                hold(S["x_ready"], t)
                pool.indirect_dma_start(stage, None, qx,
                                        bass.IndirectOffsetOnAxis(ap=row_w[:, 0:1].bitcast(I32), axis=0)).then_inc(S["stage_loaded"], 16)
                hold(S["rec_loaded"], pool.snap(n_rec) * 16)
                k = pool.snap(n_idx)
                pool.tensor_copy(idx[0][:, :], row_w[:, 1:2].bitcast(I32)).then_inc(S["idx_set"], 1)
                pool.reg_add(n_idx, n_idx, 1)
                hold(S["idx_set"], k + 1)
                hold(BIAS_USED[0], pool.snap(used[0]))
                load_records(0)

                def send():
                    with pool.If(t > 1):
                        hold(S["out_ready"], pool.snap(n_out) + 1)
                        pool.reg_add(n_out, n_out, 1)
                        pool.indirect_dma_start(out, bass.IndirectOffsetOnAxis(ap=out_idx[:, 0:1], axis=0),
                                                out_w, None).then_inc(S["out_sent"], 16)

                tile_groups(pool, n, half, between=send, reset=reset)
                hold(S["stage_loaded"], t * 16 + 16)
                hold(S["idx_set"], pool.snap(n_idx))
                pool.engine_nop().then_inc(S["row_used"], 1)
            for i in range(max(NT - 2, 0), NT):
                pool.wait_ge(S["out_ready"], i + 1)
                pool.indirect_dma_start(out, bass.IndirectOffsetOnAxis(ap=out_idx[:, 0:1], axis=0),
                                        out_w, None).then_inc(S["out_sent"], 16)
            hold(S["rec_loaded"], pool.snap(n_rec) * 16)
            pool.wait_ge(S["out_sent"], 16 * NT)

        @block.scalar
        def _(act):
            for i, to in enumerate((qx_row, kv_row)):
                for b0 in range(0, TB, 4):
                    w = min(4, TB - b0) * P
                    act.wait_ge(S["turned"], i * ((TB + 3) // 4) + b0 // 4 + 1)
                    last = act.copy(to[:, b0 * P:b0 * P + w], bank[2 * i + b0 // 4][:, 0:w])
                last.then_inc(S["turned_sb"], 1)
            act.wait_ge(S["consts_c"], 2)
            act.wait_ge(S["edges_loaded"], 32)
            act.wait_ge(S["weights_loaded"], 16 * 13)
            act.wait_ge(S["info_ready"], 1)

            with act.Fori(0, NT) as it:
                def table(j):
                    st = it * SPI + j
                    act.wait_ge(S["counted1"], st + 1)
                    act.wait_ge(S["g_done"], st)
                    act.copy(table_sb, count_ps).then_inc(S["table_ready"], 1)

                def fill(j):
                    st = it * SPI + j
                    act.wait_ge(SCAT[j % 2], (it * (SPI // 2) + j // 2) * 16 * STREAMS)
                    act.copy(rec_w[j % 2][:, :, 0:HEADS],
                             edge_sb[:, bass.ds(st * (STREAMS * HEADS), STREAMS * HEADS)].rearrange("p (s h) -> p s h", s=STREAMS)
                             )
                    act.copy(rec_w[j % 2][:, :, HEADS:HEADS + 1].rearrange("p s o -> p (s o)").bitcast(I32),
                             dst_i[:, bass.ds(st * STREAMS, STREAMS)]).then_inc(S["rec_ready"], 1)

                table(0)
                fill(0)
                act.wait_ge(S["stats1"], it + 1)
                act.activation(std[:, :], mv[:, 1:2], ACT.Sqrt, bias=eps_t[:, :]).then_inc(S["std1"], 1)
                table(1)
                fill(1)
                act.wait_ge(S["z1_turned"], it + 1)
                for c in range(KT):
                    last = act.activation(zT1[:, c * P:(c + 1) * P], turn_ps[:, c * P:(c + 1) * P], ACT.Identity,
                                          bias=ln1_cols[:, 1, c:c + 1], scale=ln1_cols[:, 0, c:c + 1])
                last.then_inc(S["z1_sb"], 1)
                for j in range(2, SPI):
                    table(j)
                    fill(j)
                for w, to in enumerate((qx_row[:, 0:C], kv_row[:, 0:C], kv_row[:, C:2 * C])):
                    act.wait_ge(S["qkv_done"], it * 3 + w + 1)
                    act.activation(to, qkv_ps[w][:, :], ACT.Copy, scale=SCALE if w == 0 else 1.0).then_inc(S["qkv_sb"], 1)
            act.drain()
            act.mul(b1_half[:, :], b1_col[:, :], 0.5).then_inc(S["phase1_act"], 1)
            act.drain()
            act.wait_ge(S["ng_out"], 16)
            used = [act.alloc_register(f"act_used{h}") for h in range(2)]
            for r in used:
                act.reg_mov(r, 0)

            def half(h, first):
                u = act.snap(used[h])
                act.wait_ge(SC[h], u + 1)
                act.activation(pr[h][:, :, :], sc[h][:, :, :], ACT.Exp).then_inc(EX[h], 1)
                act.reg_add(used[h], used[h], 1)

            def turn_att(k):
                act.wait_ge(S["att_turned"], k)
                act.copy(attT, turn_ps[:, :]).then_inc(S["att_sb"], 1)

            def turn_z2(k):
                act.wait_ge(S["stats_mid"], k)
                act.activation(std[:, :], mv[:, 1:2], ACT.Sqrt, bias=eps_t[:, :]).then_inc(S["std_mid"], 1)
                act.wait_ge(S["z2_turned"], k)
                for c in range(KT):
                    last = act.activation(z2T[:, c * P:(c + 1) * P], turn_ps[:, c * P:(c + 1) * P], ACT.Identity,
                                          bias=ln2_cols[:, 1, c:c + 1], scale=ln2_cols[:, 0, c:c + 1])
                last.then_inc(S["z2_sb"], 1)

            def hidden(k):
                act.wait_ge(S["h_done"], k)
                for c in range(HT):
                    ps = h_ps[c // 4][:, (c % 4) * P:(c % 4 + 1) * P]
                    act.activation(th[:, c * P:(c + 1) * P], ps, ACT.Tanh, bias=b1_half[:, c:c + 1], scale=0.5)
                    last = act.activation(hb[:, c * P:(c + 1) * P], ps, ACT.Identity, bias=b1_half[:, c:c + 1], scale=0.5)
                last.then_inc(S["h_act"], 1)

            def final(k):
                act.wait_ge(S["stats_end"], k)
                act.activation(std[:, :], mv[:, 1:2], ACT.Sqrt, bias=eps_t[:, :]).then_inc(S["std_end"], 1)

            with act.Fori(0, NT) as t:
                n = load_count(act, t)
                act.wait_ge(S["stage_loaded"], t * 16 + 16)
                act.wait_ge(S["q_used"], t)
                act.copy(q_w, stage[:, 0:C]).then_inc(S["q_ready"], 1)
                with act.If(t > 0):
                    turn_att(t)

                def between():
                    with act.If(t > 0):
                        turn_z2(t)
                    act.wait_ge(S["wo_done"], t)
                    act.wait_ge(S["s_ready"], t)
                    act.copy(x_w, stage[:, C:2 * C]).then_inc(S["x_ready"], 1)

                def after():
                    with act.If(t > 0):
                        hidden(t)

                tile_groups(act, n, half, between, after)
                with act.If(t > 0):
                    final(t)
            turn_att(NT)
            turn_z2(NT)
            hidden(NT)
            final(NT)

        @block.vector
        def _(dve):
            def hold(semaphore, value):
                dve.wait_ge(semaphore, value)
                dve.sem_inc(S["dve_held"], 1)

            dve.wait_ge(S["consts_a"], 3)
            dve.tensor_copy(iota_f[:, :], iota_i[:, :])
            dve.tensor_copy(part_f[:, :], part_i[:, :])
            dve.tensor_copy(rid_f[:, :], rid_i[:, :])
            dve.memset(zeros_bf[:, :], 0.0)
            dve.memset(ones[:, :], 1.0)
            dve.memset(ones_lo[:, :], 1.0)
            dve.memset(eps_t[:, :], EPS)
            dve.drain()
            dve.tensor_scalar(ident[:, :], iota_f[:, :], part_f[:, 0:1], None, ALU.is_equal)
            dve.tensor_scalar(tri[:, :], iota_f[:, :], part_f[:, 0:1], None, ALU.is_lt)
            dve.tensor_scalar(triT[:, :], iota_f[:, :], part_f[:, 0:1], None, ALU.is_gt)
            dve.wait_ge(S["src_loaded"], 16)
            dve.tensor_copy(src_f, int_a)
            dve.tensor_scalar(int_b, int_a, LO.bit_length() - 1, None, ALU.arith_shift_right)
            dve.drain()
            dve.tensor_copy(hi_f, int_b)
            dve.drain()
            dve.tensor_scalar(int_b, int_a, LO - 1, None, ALU.bitwise_and)
            dve.drain()
            dve.tensor_copy(lo_f, int_b)
            dve.drain()
            dve.drain().then_inc(S["keys_ready"], 1)

            def one_hots(b, c0):
                dve.tensor_tensor(hi_oh[b][:, :, :], hi_f[:, bass.ds(c0, STREAMS)].unsqueeze(2).broadcast_to([P, STREAMS, HI]),
                                  iota_f[:, 0:HI].unsqueeze(1).broadcast_to([P, STREAMS, HI]), ALU.is_equal)
                return dve.tensor_tensor(lo_oh[b][:, :, :], lo_f[:, bass.ds(c0, STREAMS)].unsqueeze(2).broadcast_to([P, STREAMS, LO]),
                                         iota_f[:, 0:LO].unsqueeze(1).broadcast_to([P, STREAMS, LO]), ALU.is_equal)

            with dve.Fori(0, STEPS // 2) as i:
                for b in range(2):
                    dve.wait_ge(S["onehots_free"], i * 2 + b + 1)
                    one_hots(b, (i * 2 + b) * STREAMS).then_inc(S["onehots_ready"], 1)

            dve.wait_ge(S["hist_done"], 1)
            dve.tensor_copy(hist[:, :, :].rearrange("h s l -> h (s l)"), count_ps)
            dve.drain()
            dve.tensor_reduce(deg[:, :], hist[:, :, :].rearrange("h s l -> h l s"), AX.X, ALU.add)
            dve.drain()
            dve.tensor_scalar(deg_i[:, :], deg[:, :], float(GROUP - 1), None, ALU.add)
            dve.drain()
            dve.tensor_scalar(nb_i[:, :], deg_i[:, :], GROUP.bit_length() - 1, None, ALU.arith_shift_right)
            dve.drain()
            dve.tensor_scalar(width[:, :], nb_i[:, :], 1.0, None, ALU.add)
            dve.drain()
            dve.tensor_tensor_scan(cum[:, :], ones_lo[:, :], width[:, :], 0.0, ALU.mult, ALU.add)
            dve.drain()
            dve.tensor_copy(offs[:, :], cum[:, LO - 1:LO]).then_inc(S["prefix_in"], 1)
            dve.tensor_tensor(blk[:, :], cum[:, :], width[:, :], ALU.subtract)
            dve.drain()
            dve.wait_ge(S["prefix_out"], 1)
            dve.tensor_scalar(blk[:, :], blk[:, :], turn_ps[0:HI, 0:1], None, ALU.add)
            dve.drain()
            dve.tensor_scalar(start_tab[:, 0, :], blk[:, :], float(GROUP), None, ALU.mult)
            dve.drain()
            for s in range(1, STREAMS):
                dve.tensor_tensor(start_tab[:, s, :], start_tab[:, s - 1, :], hist[:, s - 1, :], ALU.add)
                dve.drain()
            dve.tensor_copy(info_w[:, :, 0].bitcast(I32), rid_i[:, :])
            dve.tensor_copy(info_w[:, :, 1].bitcast(I32), blk[:, :])
            dve.tensor_tensor(info_w[:, :, 2], blk[:, :], nb_i[:, :], ALU.add)
            dve.tensor_copy(info_w[:, :, 3], nb_i[:, :])
            dve.tensor_scalar(key_w[:, :], nb_i[:, :], 2047.0, float(L), ALU.min, ALU.mult)
            dve.drain()
            dve.tensor_tensor(key_w[:, :], key_w[:, :], rid_f[:, :], ALU.subtract)
            dve.drain().then_inc(S["info_ready"], 1)

            dve.wait_ge(S["keys_loaded"], 48)
            with dve.Fori(0, NT) as it:
                def step(j):
                    st = it * SPI + j
                    b = j % 2
                    dve.wait_ge(SRCB[b], (it * (SPI // 2) + j // 2 + 1) * 32)
                    dve.tensor_scalar(hitT[b], hib[b], part_f[0:HI, 0:1], None, ALU.is_equal).then_inc(S["hit_ready"], 1)
                    dve.wait_ge(S["counted1"], st)
                    one_hots(b, st * STREAMS).then_inc(S["oh1_ready"], 1)
                    dve.drain()
                    for s in range(STREAMS):
                        last = dve.scalar_tensor_tensor(eq[:, s * P:(s + 1) * P], srcb[b][:, s * P:(s + 1) * P],
                                                        src_f[:, bass.ds(st * STREAMS + s, 1)], tri[:, :],
                                                        ALU.is_equal, ALU.mult, accum_out=rank_w[:, s:s + 1])
                    last.then_inc(S["srcb_used"], 1)
                    dve.wait_ge(S["g_done"], st + 1)
                    dve.tensor_tensor(sel, sel_ps[:, :], lo_oh[b][:, :, :].rearrange("p s l -> p (s l)"), ALU.mult).then_inc(S["sel_free"], 1)
                    dve.drain()
                    dve.tensor_reduce(base_w[:, :], sel.rearrange("p (s l) -> p s l", s=STREAMS), AX.X, ALU.add)
                    dve.drain()
                    dve.wait_ge(SCAT[b], (it * (SPI // 2) + j // 2) * 16 * STREAMS)
                    dve.tensor_tensor(pos_i[b][:, :], base_w[:, :], rank_w[:, :], ALU.add).then_inc(S["pos_ready"], 1)

                step(0)
                dve.wait_ge(S["x_loaded"], it * 16 + 16)
                dve.bn_stats(stats[:, :], qx_row[:, C:2 * C])
                dve.drain()
                dve.bn_aggr(mv[:, :], stats[:, :]).then_inc(S["stats1"], 1)
                dve.tensor_scalar(greater, keys_all, key_col[:, bass.ds(it, 1)], 0.0, ALU.is_gt, ALU.add,
                                  accum_out=rank_f[:, bass.ds(it, 1)])
                dve.wait_ge(S["std1"], it + 1)
                dve.reciprocal(rstd[:, :], std[:, :])
                dve.drain()
                dve.wait_ge(S["z1_turned"], it)
                dve.tensor_scalar(z1, qx_row[:, C:2 * C], mv[:, 0:1], rstd[:, 0:1], ALU.subtract, ALU.mult).then_inc(S["z1_ready"], 1)
                for j in range(1, SPI):
                    step(j)
            dve.drain()
            dve.tensor_copy(rank_i[:, :], rank_f[:, :]).then_inc(S["rank_ready"], 1)
            dve.drain().then_inc(S["phase1_dve"], 1)
            dve.wait_ge(S["ranked_loaded"], 32)
            dve.tensor_reduce(ng_f[:, :], ranked_sb[:, :, 3], AX.X, ALU.max)
            dve.drain()
            dve.tensor_scalar(ng_i[:, :], ng_f[:, :], 1.0, None, ALU.max).then_inc(S["ng_ready"], 1)
            dve.wait_ge(S["ng_out"], 16)
            dve.wait_ge(S["qkv_out"], 32 * NT)
            used = [dve.alloc_register(f"dve_used{h}") for h in range(2)]
            loads = [dve.alloc_register(f"dve_loads{h}") for h in range(2)]
            n_out = dve.alloc_register("dve_outs")
            n_resets = dve.alloc_register("dve_resets")
            for r in (*used, *loads, n_out, n_resets):
                dve.reg_mov(r, 0)

            def reset():
                with dve.If(dve.snap(loads[0]) > RESET_AT):
                    dve.reg_add(n_resets, n_resets, 1)
                    dve.drain().then_inc(S["quiet"], 1)
                    hold(S["restarted"], dve.snap(n_resets))
                    for r in loads:
                        dve.reg_mov(r, 0)

            def heads(ap):
                return ap.rearrange("p (h d) -> p h d", h=HEADS)

            def rescale(h, u):
                dve.tensor_tensor(heads(acc), heads(acc), pr[h][:, GROUP, :].unsqueeze(2).broadcast_to([P, HEADS, D]), ALU.mult)
                for a in range(2):
                    hold(PES[h][a], u)
                dve.drain()
                dve.tensor_tensor(acc, acc, pv_ps[h][:, :], ALU.add).then_inc(PV_FREE[h], 1)
                dve.drain()

            def half(h, first):
                u = dve.snap(used[h])
                loaded = dve.snap(loads[h]) * (16 * SUB) + 16 * SUB
                s_all = sc[h][:, 0:GROUP, :]
                for a in range(2):
                    part_kv = KV[h][:, a * SUB:(a + 1) * SUB, 0:C]
                    prod = prods[:, a * SUB:(a + 1) * SUB, :]
                    dve.wait_ge(KVS[h][a], loaded)
                    dve.tensor_tensor(prod, part_kv, q_w.unsqueeze(1).broadcast_to([P, SUB, C]), ALU.mult)
                    dve.drain()
                    dve.tensor_reduce(sc[h][:, a * SUB:(a + 1) * SUB, :], prod.rearrange("p s (h d) -> p s h d", h=HEADS), AX.X, ALU.add)
                dve.drain()
                dve.tensor_tensor(s_all, s_all, rec[h][:, :, 0:HEADS], ALU.add).then_inc(BIAS_USED[h], 1)
                dve.drain()
                dve.tensor_reduce(m_new[:, :], s_all.rearrange("p s h -> p h s"), AX.X, ALU.max)
                dve.drain()
                dve.tensor_tensor(m_new[:, :], m_new[:, :], m_run[:, :], ALU.max)
                dve.drain()
                dve.tensor_tensor(s_all, s_all, m_new[:, :].unsqueeze(1).broadcast_to([P, GROUP, HEADS]), ALU.subtract)
                dve.tensor_tensor(sc[h][:, GROUP, :], m_run[:, :], m_new[:, :], ALU.subtract).then_inc(SC[h], 1)
                dve.drain()
                dve.tensor_copy(m_run[:, :], m_new[:, :])
                if not first:
                    rescale(1 - h, dve.snap(used[1 - h]))
                dve.wait_ge(EX[h], u + 1)
                for a in range(2):
                    part_kv = KV[h][:, a * SUB:(a + 1) * SUB, C:2 * C].rearrange("p s (h d) -> p s h d", h=HEADS)
                    dve.tensor_tensor(part_kv, part_kv,
                                      pr[h][:, a * SUB:(a + 1) * SUB, :].unsqueeze(3).broadcast_to([P, SUB, HEADS, D]),
                                      ALU.mult).then_inc(PVS[h][a], 1)
                dve.tensor_reduce(l_sum[:, :], pr[h][:, 0:GROUP, :].rearrange("p s h -> p h s"), AX.X, ALU.add)
                dve.tensor_tensor(l_run[:, :], l_run[:, :], pr[h][:, GROUP, :], ALU.mult)
                dve.drain()
                dve.tensor_tensor(l_run[:, :], l_run[:, :], l_sum[:, :], ALU.add)
                dve.reg_add(used[h], used[h], 1)
                dve.reg_add(loads[h], loads[h], 1)

            def norm_parts(stats_sem, std_sem, k):
                dve.drain()
                dve.bn_aggr(mv[:, :], stats[:, :]).then_inc(stats_sem, 1)
                dve.wait_ge(std_sem, k)
                dve.reciprocal(rstd[:, :], std[:, :])
                dve.drain()

            def residual(k):
                dve.wait_ge(S["wo_done"], k)
                dve.wait_ge(S["x_ready"], k)
                dve.bn_stats(stats[:, :], wo_ps[:, :])
                norm_parts(S["stats_mid"], S["std_mid"], k)
                dve.tensor_scalar(z2, wo_ps[:, :], mv[:, 0:1], rstd[:, 0:1], ALU.subtract, ALU.mult).then_inc(S["z2_ready"], 1)
                dve.tensor_tensor(s_w, wo_ps[:, :], x_w, ALU.add).then_inc(S["s_ready"], 1)

            def silu(k):
                dve.wait_ge(S["h_act"], k)
                dve.scalar_tensor_tensor(hT, th, 1.0, hb, ALU.add, ALU.mult).then_inc(S["h_ready"], 1)

            def last_norm(k):
                dve.wait_ge(S["y_done"], k)
                dve.bn_stats(stats[:, :], y_ps[:, :])
                norm_parts(S["stats_end"], S["std_end"], k)
                dve.wait_ge(S["out_sent"], dve.snap(n_out) * 16)
                dve.reg_add(n_out, n_out, 1)
                dve.tensor_copy(out_idx[:, :], perm[:, bass.ds(k, 1)].bitcast(I32))
                dve.tensor_scalar(out_w, y_ps[:, :], mv[:, 0:1], rstd[:, 0:1], ALU.subtract, ALU.mult)
                dve.drain().then_inc(S["out_ready"], 1)

            with dve.Fori(0, NT) as t:
                n = load_count(dve, t)
                dve.drain()
                dve.memset(m_run[:, :], FLOOR)
                dve.memset(l_run[:, :], 0.0)
                dve.memset(acc, 0.0)
                dve.drain()
                hold(S["q_ready"], t + 1)

                def between():
                    with dve.If(t > 0):
                        residual(t)

                def after():
                    with dve.If(t > 0):
                        silu(t)

                tile_groups(dve, n, half, between, after, reset)
                dve.drain().then_inc(S["q_used"], 1)
                with dve.If(t > 0):
                    last_norm(t)
                with dve.If(n % 2 > 0):
                    rescale(0, dve.snap(used[0]))
                with dve.Else():
                    rescale(1, dve.snap(used[1]))
                dve.tensor_scalar(l_inv[:, :], l_run[:, :], TINY, None, ALU.max)
                dve.drain()
                dve.reciprocal(l_inv[:, :], l_inv[:, :])
                dve.drain()
                dve.wait_ge(S["att_turned"], t)
                dve.tensor_tensor(heads(att), heads(acc), l_inv[:, :].unsqueeze(2).broadcast_to([P, HEADS, D]), ALU.mult).then_inc(S["att_ready"], 1)
            residual(NT)
            silu(NT)
            last_norm(NT)

        @block.tensor
        def _(pe):
            pe.wait_ge(S["keys_ready"], 1)
            for i, of in enumerate((src_f, hi_f)):
                for b in range(TB):
                    last = pe.transpose(bank[2 * i + b // 4][:, (b % 4) * P:(b % 4 + 1) * P], of[:, b * P:(b + 1) * P], ident[:, :])
                    if b % 4 == 3 or b == TB - 1:
                        last.then_inc(S["turned"], 1)
            pe.wait_ge(S["turned_sb"], 2)
            pe.matmul(count_ps, zeros_bf[:, 0:HI], zeros_bf[:, :], start=True, stop=True)
            pe.sem_inc(S["onehots_free"], 2)
            pe.sem_inc(S["srcb_used"], 2)

            def count(b):
                for s in range(STREAMS):
                    last = pe.matmul(count_ps[:, s * LO:(s + 1) * LO], hi_oh[b][:, s, :], lo_oh[b][:, s, :],
                                     start=False, stop=True, skip_group_check=True)
                return last

            with pe.Fori(0, STEPS // 2) as i:
                for b in range(2):
                    pe.wait_ge(S["onehots_ready"], i * 2 + b + 1)
                    count(b).then_inc(S["onehots_free"], 1)
            pe.wait_ge(S["onehots_free"], STEPS + 2)
            pe.sem_inc(S["hist_done"], 1)
            pe.wait_ge(S["prefix_in"], 1)
            pe.matmul(turn_ps[0:HI, 0:1], triT[0:HI, 0:HI], offs[:, :], start=True, stop=True).then_inc(S["prefix_out"], 1)
            pe.wait_ge(S["info_ready"], 1)
            pe.matmul(count_ps, ident[0:HI, 0:HI], start_tab[:, :, :].rearrange("h s l -> h (s l)"),
                      start=True, stop=True).then_inc(S["counted1"], 1)
            pe.wait_ge(S["weights_loaded"], 16 * 13)

            with pe.Fori(0, NT) as it:
                def step(j):
                    st = it * SPI + j
                    b = j % 2
                    pe.wait_ge(S["hit_ready"], st + 1)
                    pe.wait_ge(S["table_ready"], st + 1)
                    pe.wait_ge(S["sel_free"], st)
                    for s in range(STREAMS):
                        last = pe.matmul(sel_ps[:, s * LO:(s + 1) * LO], hitT[b][:, s * P:(s + 1) * P],
                                         table_sb[:, s * LO:(s + 1) * LO], start=True, stop=True)
                    last.then_inc(S["g_done"], 1)
                    pe.wait_ge(S["oh1_ready"], st + 1)
                    count(b).then_inc(S["counted1"], 1)

                step(0)
                step(1)
                pe.wait_ge(S["z1_ready"], it + 1)
                for c in range(KT):
                    last = pe.transpose(turn_ps[:, c * P:(c + 1) * P], z1[:, c * P:(c + 1) * P], ident[:, :])
                last.then_inc(S["z1_turned"], 1)
                pe.wait_ge(S["z1_sb"], it + 1)
                for w in range(3):
                    pe.wait_ge(S["qkv_sb"], it * 3)
                    pe.matmul(qkv_ps[w][:, :], ones[:, :], bias3[:, w * C:(w + 1) * C], start=True, stop=False)
                    for c in range(KT):
                        last = pe.matmul(qkv_ps[w][:, :], zT1[:, c * P:(c + 1) * P], Wqkv[:, w, c, :],
                                         start=False, stop=c == KT - 1)
                    last.then_inc(S["qkv_done"], 1)
                for j in range(2, SPI):
                    step(j)
            pe.wait_ge(S["qkv_done"], 3 * NT)
            pe.sem_inc(S["phase1_pe"], 1)
            pe.wait_ge(S["qkv_sb"], 3 * NT)
            pe.wait_ge(S["sel_free"], STEPS)
            pe.wait_ge(S["weights2"], 48)
            pe.wait_ge(S["ng_out"], 16)
            used = [pe.alloc_register(f"pe_used{h}") for h in range(2)]
            for r in used:
                pe.reg_mov(r, 0)
            for h in range(2):
                pe.sem_inc(PV_FREE[h], 1)

            def half(h, first):
                u = pe.snap(used[h])
                pe.wait_ge(PV_FREE[h], u + 1)
                for a in range(2):
                    pe.wait_ge(PVS[h][a], u + 1)
                    for s in range(a * SUB, (a + 1) * SUB):
                        last = pe.matmul(pv_ps[h][:, :], ident[:, :], KV[h][:, s, C:2 * C],
                                         start=s == 0, stop=s == GROUP - 1)
                    last.then_inc(PES[h][a], 1)
                pe.reg_add(used[h], used[h], 1)

            def out_proj(k):
                pe.wait_ge(S["att_ready"], k)
                for c in range(KT):
                    last = pe.transpose(turn_ps[:, c * P:(c + 1) * P], att[:, c * P:(c + 1) * P], ident[:, :])
                last.then_inc(S["att_turned"], 1)
                pe.matmul(wo_ps[:, :], ones[:, :], bias2[:, 0:C], start=True, stop=False)
                pe.wait_ge(S["x_ready"], k)
                pe.matmul(wo_ps[:, :], ident[:, :], x_w, start=False, stop=False)
                pe.wait_ge(S["att_sb"], k)
                for c in range(KT):
                    last = pe.matmul(wo_ps[:, :], attT[:, c * P:(c + 1) * P], Wo_sb[:, c, :], start=False, stop=c == KT - 1)
                last.then_inc(S["wo_done"], 1)

            def up(k):
                pe.wait_ge(S["z2_ready"], k)
                for c in range(KT):
                    last = pe.transpose(turn_ps[:, c * P:(c + 1) * P], z2[:, c * P:(c + 1) * P], ident[:, :])
                last.then_inc(S["z2_turned"], 1)
                pe.wait_ge(S["z2_sb"], k)
                for m in range(HT):
                    for c in range(KT):
                        last = pe.matmul(h_ps[m // 4][:, (m % 4) * P:(m % 4 + 1) * P], W1_sb[:, c, m * P:(m + 1) * P],
                                         z2T[:, c * P:(c + 1) * P], start=c == 0, stop=c == KT - 1)
                last.then_inc(S["h_done"], 1)

            def down(k):
                pe.matmul(y_ps[:, :], ones[:, :], bias2[:, C:2 * C], start=True, stop=False)
                pe.wait_ge(S["s_ready"], k)
                pe.matmul(y_ps[:, :], ident[:, :], s_w, start=False, stop=False)
                pe.wait_ge(S["h_ready"], k)
                for m in range(HT):
                    last = pe.matmul(y_ps[:, :], hT[:, m * P:(m + 1) * P], W2_sb[:, m, :], start=False, stop=m == HT - 1)
                last.then_inc(S["y_done"], 1)

            with pe.Fori(0, NT) as t:
                n = load_count(pe, t)
                with pe.If(t > 0):
                    out_proj(t)

                def between():
                    with pe.If(t > 0):
                        up(t)

                def after():
                    with pe.If(t > 0):
                        down(t)

                tile_groups(pe, n, half, between, after)
            out_proj(NT)
            up(NT)
            down(NT)


_INS = ["x", "src", "dst", "edge_attr_8"] + ["L0_gnn_" + n for n in (
    "Wq", "bq", "Wk", "bk", "Wv", "bv", "Wo", "bo", "ln1_g", "ln1_b", "ln2_g", "ln2_b", "W1", "b1", "W2", "b2")]


def kernel(**inputs):
    import numpy as _np
    import concourse.bacc as _bacc
    from concourse import mybir as _mybir
    from concourse.bass_utils import run_bass_kernel_spmd as _run

    nc = _bacc.Bacc("TRN2", target_bir_lowering=False, num_devices=1)
    arrays, args = {}, []
    for name in _INS:
        a = _np.ascontiguousarray(inputs[name])
        arrays[f"in_{name}_dram"] = a
        args.append(nc.dram_tensor(f"in_{name}_dram", a.shape, _mybir.dt.from_np(a.dtype), kind="ExternalInput").ap())
    shape = inputs["x"].shape
    args.append(nc.dram_tensor("out_0_dram", shape, _mybir.dt.float32, kind="ExternalOutput").ap())
    layer_kernel(nc, *args)
    r = _run(nc, [arrays], core_ids=[0])
    return r.results[0]["out_0_dram"]
```

```python
from contextlib import ExitStack

import concourse.bass as bass
from concourse import mybir

F32 = mybir.dt.float32
BF16 = mybir.dt.bfloat16
I32 = mybir.dt.int32
ALU = mybir.AluOpType
ACT = mybir.ActivationFunctionType
AX = mybir.AxisListType

P = 128
HEADS = 8
GROUP = 8
SUB = GROUP // 2
STREAMS = 8
REC = 12
LO = 64
EPS = 1e-5
PAIRS = GROUP // 2
PEEL = 5
PAD_BIAS = -3.0e38
FLOOR = -1.0e38
TINY = 1.0e-30
RESET_AT = 400
NO_COL = 1 << 20


def layer_kernel(nc, x, src, dst, edge_bias, Wq, bq, Wk, bk, Wv, bv, Wo, bo, ln1_g, ln1_b,
                 ln2_g, ln2_b, W1, b1, W2, b2, out):
    L, C = x.shape
    E = src.shape[0]
    HID = W1.shape[1]
    D = C // HEADS
    NT = L // P
    KT = C // P
    HT = HID // P
    HI = L // LO
    COLS = E // P
    STEPS = COLS // STREAMS
    SPI = STEPS // NT
    TB = COLS // P
    RPP = L // P
    NBLK = E // GROUP + 2 * L
    SH = SUB * HEADS
    FOLD = P // SH
    PADN = 96
    SCALE = float(D) ** -0.5
    assert HT == 8 and FOLD == 4 and D % FOLD == 0 and NT > 1
    assert SPI % 2 == 0 and SPI * NT == STEPS and (NBLK * GROUP) % (P * PADN) == 0

    srcT = nc.dram_tensor("srcT", [COLS, P], F32, kind="Internal").ap()
    hiT = nc.dram_tensor("hiT", [COLS, P], F32, kind="Internal").ap()
    records = nc.dram_tensor("records", [NBLK * GROUP, REC], F32, kind="Internal").ap()
    row_info = nc.dram_tensor("row_info", [L, 4], F32, kind="Internal").ap()
    row_key = nc.dram_tensor("row_key", [L], F32, kind="Internal").ap()
    rows_ranked = nc.dram_tensor("rows_ranked", [L, 4], F32, kind="Internal").ap()
    n_groups = nc.dram_tensor("n_groups", [1, NT], I32, kind="Internal").ap()
    qx = nc.dram_tensor("qx", [L, 2 * C], F32, kind="Internal").ap()
    kv = nc.dram_tensor("kv", [L, 2 * C], F32, kind="Internal").ap()
    blocks = records.rearrange("(n g) r -> n (g r)", g=GROUP)

    with ExitStack() as ctx:
        def sb(name, shape, dt=F32):
            return ctx.enter_context(nc.sbuf_tensor(name, shape, dt))

        def sem(name):
            return ctx.enter_context(nc.semaphore(name))

        region_a = sb("region_a", [P, 2 * GROUP * 2 * C])
        KV = [region_a[:, h * GROUP * 2 * C:(h + 1) * GROUP * 2 * C].rearrange("p (s c) -> p s c", s=GROUP)
              for h in range(2)]
        edge_sb = region_a[:, 0:COLS * HEADS]
        at = COLS * HEADS
        src_f, hi_f, lo_f = (region_a[:, at + i * COLS:at + (i + 1) * COLS] for i in range(3))
        int_a, int_b, dst_i = (region_a[:, at + i * COLS:at + (i + 1) * COLS].bitcast(I32) for i in range(3, 6))
        x_in = region_a[:, COLS * (HEADS + 6):COLS * (HEADS + 6) + C]
        region_b = sb("region_b", [P, KT * C + KT * HID + HT * C])
        Wqkv = region_b[:, 0:3 * KT * C].rearrange("p (w k n) -> p w k n", w=3, k=KT)
        keys_all = region_b[:, 3 * KT * C:3 * KT * C + L]
        Wo_sb = region_b[:, 0:KT * C].rearrange("p (k n) -> p k n", k=KT)
        W1_sb = region_b[:, KT * C:KT * C + KT * HID].rearrange("p (k n) -> p k n", k=KT)
        W2_sb = region_b[:, KT * C + KT * HID:].rearrange("p (k n) -> p k n", k=HT)
        region_c = sb("region_c", [P, 14080])
        pos_c = [0]

        def part(words):
            v = region_c[:, pos_c[0]:pos_c[0] + words]
            pos_c[0] += words
            return v

        srcb = [part(STREAMS * P) for _ in range(2)]
        hib = [part(STREAMS * P)[0:HI, :] for _ in range(2)]
        hitT = [part(STREAMS * P)[0:HI, :] for _ in range(2)]
        sel = part(STREAMS * LO)
        eq = part(STREAMS * P // 2).bitcast(BF16)
        table_sb = part(STREAMS * LO)[0:HI, :]
        qx_row, kv_row = part(2 * C), part(2 * C)
        z1, zT1 = part(C), part(C)
        greater = part(L // 2).bitcast(BF16)
        used_sort = pos_c[0]
        pos_c[0] = 0
        q_w, x_bo, x_b2, row_qx = part(C), part(C), part(C), part(2 * C)
        acc, att, attT = part(C), part(C), part(C)
        s_w, z2, z2T, out_w = part(C), part(C), part(C), part(C)
        th, hb, hT = part(HID), part(HID), part(HID)
        prods = part(GROUP * C).rearrange("p (s c) -> p s c", s=GROUP)
        scT_sb, vT_sb = part(2 * P), part(C)
        assert max(used_sort, pos_c[0]) <= 14080

        pad_rec = sb("pad_rec", [P, PADN, REC])
        rec_w = [sb(f"rec_w{i}", [P, STREAMS, REC]) for i in range(2)]
        hi_oh = [sb(f"hi_oh{i}", [P, STREAMS, HI], BF16) for i in range(2)]
        lo_oh = [sb(f"lo_oh{i}", [P, STREAMS, LO], BF16) for i in range(2)]
        rank_w = sb("rank_w", [P, STREAMS])
        base_w = sb("base_w", [P, STREAMS])
        pos_i = [sb(f"pos_i{i}", [P, STREAMS], I32) for i in range(2)]
        iota_i = sb("iota_i", [P, P], I32)
        iota_f = sb("iota_f", [P, P])
        part_i = sb("part_i", [P, 1], I32)
        part_f = sb("part_f", [P, 1])
        ident = sb("ident", [P, P])
        tri = sb("tri", [P, P])
        triT = sb("triT", [P, P])
        fold = sb("fold", [P, SH])
        quarter_f = sb("quarter_f", [P, 1])
        quarter_i = sb("quarter_i", [P, 1], I32)
        ones = sb("ones", [1, P])
        zeros_bf = sb("zeros_bf", [P, STREAMS * LO], BF16)
        eps_t = sb("eps_t", [P, 1])
        hist = sb("hist", [HI, STREAMS, LO])
        start_tab = sb("start_tab", [HI, STREAMS, LO])
        deg = sb("deg", [HI, LO])
        deg_i = sb("deg_i", [HI, LO], I32)
        nb_i = sb("nb_i", [HI, LO], I32)
        width = sb("width", [HI, LO])
        cum = sb("cum", [HI, LO])
        blk = sb("blk", [HI, LO])
        ones_lo = sb("ones_lo", [HI, LO])
        rid_i = sb("rid_i", [HI, LO], I32)
        rid_f = sb("rid_f", [HI, LO])
        key_w = sb("key_w", [HI, LO])
        info_w = sb("info_w", [HI, LO, 4])
        offs = sb("offs", [HI, 1])
        key_col = sb("key_col", [P, RPP])
        rank_f = sb("rank_f", [P, RPP])
        rank_i = sb("rank_i", [P, RPP], I32)
        info_sb = sb("info_sb", [P, RPP, 4])
        ranked_sb = sb("ranked_sb", [NT, P, 4])
        ng_f = sb("ng_f", [NT, 1])
        ng_i = sb("ng_i", [NT, 1], I32)
        bias3 = sb("bias3", [1, 3 * C])
        bo_all = sb("bo_all", [P, C])
        b2_all = sb("b2_all", [P, C])
        ln1_cols = sb("ln1_cols", [P, 2, KT])
        ln2_cols = sb("ln2_cols", [P, 2, KT])
        b1_col = sb("b1_col", [P, HT])
        b1_half = sb("b1_half", [P, HT])
        stats = sb("stats", [P, 6])
        mv = sb("mv", [P, 2])
        std = sb("std", [P, 1])
        rstd = sb("rstd", [P, 1])
        perm = sb("perm", [P, NT + 2])
        row_next = sb("row_next", [P, 4])
        row_w = sb("row_w", [P, 4])
        idx = [sb(f"idx{i}", [P, 1], I32) for i in range(2)]
        out_idx = sb("out_idx", [P, 1], I32)
        rec = [sb(f"rec{i}", [P, GROUP, REC]) for i in range(2)]
        bias_w = [sb(f"bias_w{i}", [P, GROUP, HEADS]) for i in range(2)]
        cols = [sb(f"cols{i}", [P, GROUP]) for i in range(2)]
        sc = [sb(f"sc{i}", [P, GROUP + 1, HEADS]) for i in range(2)]
        pr = [sb(f"pr{i}", [P, GROUP + 1, HEADS]) for i in range(2)]
        m_run = sb("m_run", [P, HEADS])
        m_new = sb("m_new", [P, HEADS])
        l_run = sb("l_run", [P, HEADS])
        l_sum = sb("l_sum", [P, HEADS])
        l_inv = sb("l_inv", [P, HEADS])

        bank = [ctx.enter_context(nc.psum_tensor(f"bank{i}", [P, 512], F32)) for i in range(8)]
        count_ps = bank[0][0:HI, :]
        sel_ps = [bank[1], bank[6]]
        turn_ps = bank[2]
        qkv_ps = bank[3:6]
        scT_ps, sc_ps = bank[0][:, 0:2 * P], bank[4][:, 0:2 * SH]
        vT_ps, acc_ps = bank[1], bank[7]
        wo_ps = y_ps = bank[3]
        h_ps = bank[5:7]

        names = """kv00 kv01 kv02 kv03 kv10 kv11 kv12 kv13 rec_loaded src_loaded edges_loaded weights_loaded consts_a pad_ready
            table_cleared keys_ready turned turned_sb turned_out onehots_free onehots_ready hist_done prefix_in
            prefix_out info_ready info_out keys_loaded srcb0 srcb1 srcb_used hit_ready g_done sel_free oh1_ready
            counted1 table_ready pos_ready rec_ready scat0 scat1 x_loaded stats1 std1 z1_ready z1_turned z1_sb x_out
            qkv_done qkv_sb qkv_out rank_ready ranked ranked_loaded ng_ready ng_out phase1_dve phase1_act
            phase1_pe weights2 row_loaded row_used qx_loaded x_ready idx_set prods_ready scT_ready
            scT_sb_ready sc_summed sc_ready p_ready v_dve v_act y_taken summed vT_sb_ready acc_ready acc_taken
            att_ready att_turned
            att_sb wo_done z2_ready z2_turned z2_sb h_done0 h_done1 h_act0 h_act1 h_ready0 h_ready1 q_taken y_done out_ready out_sent consts_c
            s_ready quiet restarted pool_held dve_held sp_held stats_end stats_mid std_end std_mid""".split()
        S = {n: sem(n) for n in names}
        SRCB = [S["srcb0"], S["srcb1"]]
        SCAT = [S["scat0"], S["scat1"]]
        DMA_COUNTS = [S[n] for n in ("kv00", "kv01", "kv02", "kv03", "kv10", "kv11", "kv12", "kv13", "rec_loaded")]
        H_ACT, H_READY = [S["h_act0"], S["h_act1"]], [S["h_ready0"], S["h_ready1"]]
        H_DONE = [S["h_done0"], S["h_done1"]]
        KVS = [[S[f"kv{h}{pair}"] for pair in range(PAIRS)] for h in range(2)]
        block = ctx.enter_context(nc.Block())

        def load_count(eng, t):
            return eng.value_load(n_groups[0:1, bass.ds(t, 1)], min_val=1, max_val=NBLK)

        def next_count(eng, t, count):
            with eng.If(t < NT - 1):
                nxt = nc.s_assert_within(t + 1, 1, NT - 1, skip_runtime_bounds_check_because="the If has t < NT - 1")
                eng.reg_mov(count, load_count(eng, nxt))

        def tile_groups(eng, n, f, body, alone, reset=None):
            body(f, 0)
            for g in range(1, PEEL):
                with eng.If(n > g):
                    body((f + g) % 2, g)
                with eng.Else():
                    alone(g)
            assert PEEL % 2
            with eng.If(n > PEEL):
                with eng.Fori(PEEL // 2, n // 2) as i:
                    if reset:
                        reset()
                    body(1 - f, PEEL)
                    with eng.If(n > i * 2 + 2):
                        body(f, PEEL)

        def by_half(eng, groups, tile):
            with eng.If(eng.snap(groups) % 2 > 0):
                tile(1)
            with eng.Else():
                tile(0)

        @block.sync
        def _(sp):
            sp.dma_start(int_a, src.rearrange("(p c) -> p c", p=P)).then_inc(S["src_loaded"], 16)
            sp.dma_start(dst_i, dst.rearrange("(p c) -> p c", p=P)).then_inc(S["edges_loaded"], 16)
            sp.dma_start(edge_sb, edge_bias.rearrange("(p c) h -> p (c h)", p=P)).then_inc(S["edges_loaded"], 16)
            sp.wait_ge(S["pad_ready"], 3)
            flat = records.rearrange("(n p k) r -> n p (k r)", p=P, k=PADN)
            for n in range(flat.shape[0]):
                sp.dma_start(flat[n], pad_rec[:, :, :].rearrange("p k r -> p (k r)")).then_inc(S["table_cleared"], 16)
            for w, W in enumerate((Wq, Wk, Wv)):
                sp.dma_start(Wqkv[:, w], W.rearrange("(k p) n -> p k n", p=P)).then_inc(S["weights_loaded"], 16)
            for w, b in enumerate((bq, bk, bv)):
                sp.dma_start(bias3[:, w * C:(w + 1) * C], b.rearrange("(a n) -> a n", a=1)).then_inc(S["weights_loaded"], 16)
            for to, b in ((bo_all, bo), (b2_all, b2)):
                sp.dma_start(to[:, :], b.rearrange("(a n) -> a n", a=1).broadcast_to([P, C])).then_inc(S["weights_loaded"], 16)
            with nc.allow_non_contiguous_dma(reason="vectors of a few KB to columns"):
                for to, (g, b) in ((ln1_cols, (ln1_g, ln1_b)), (ln2_cols, (ln2_g, ln2_b))):
                    sp.dma_start(to[:, 0, :], g.rearrange("(k p) -> p k", p=P)).then_inc(S["weights_loaded"], 16)
                    sp.dma_start(to[:, 1, :], b.rearrange("(k p) -> p k", p=P)).then_inc(S["weights_loaded"], 16)
                sp.dma_start(b1_col[:, :], b1.rearrange("(k p) -> p k", p=P)).then_inc(S["weights_loaded"], 16)
            sp.wait_ge(S["turned_sb"], 2)
            for to, of in ((srcT, qx_row), (hiT, kv_row)):
                sp.dma_start(to.rearrange("(b c) e -> c b e", c=P),
                             of[:, 0:COLS].rearrange("p (b e) -> p b e", b=TB)).then_inc(S["turned_out"], 16)
            sp.wait_ge(S["info_ready"], 1)
            sp.dma_start(row_info.rearrange("(h l) w -> h (l w)", h=HI),
                         info_w[:, :, :].rearrange("h l w -> h (l w)")).then_inc(S["info_out"], 16)
            sp.dma_start(row_key.rearrange("(h l) -> h l", h=HI), key_w[:, :]).then_inc(S["info_out"], 16)
            sp.wait_ge(S["info_out"], 32)
            sp.dma_start(info_sb[:, :, :], row_info.rearrange("(p j) w -> p j w", p=P)).then_inc(S["keys_loaded"], 16)
            sp.dma_start(key_col[:, :], row_key.rearrange("(p j) -> p j", p=P)).then_inc(S["keys_loaded"], 16)
            sp.dma_start(keys_all, row_key.rearrange("(a n) -> a n", a=1).broadcast_to([P, L])).then_inc(S["keys_loaded"], 16)
            sp.wait_ge(S["turned_out"], 32)
            chunk = srcT.rearrange("(s c) e -> s (c e)", c=STREAMS)
            chunk_hi = hiT.rearrange("(s c) e -> s (c e)", c=STREAMS)
            def load_chunks(st, b):
                sp.wait_ge(S["srcb_used"], st + 1)
                sp.dma_start(srcb[b], chunk[bass.ds(st, 1), :].broadcast_to([P, STREAMS * P])).then_inc(SRCB[b], 16)
                sp.dma_start(hib[b], chunk_hi[bass.ds(st, 1), :].broadcast_to([HI, STREAMS * P])).then_inc(SRCB[b], 16)

            sp.dma_start(x_in, x[0:P, :]).then_inc(S["x_loaded"], 16)
            for b in range(2):
                load_chunks(b, b)
            with sp.Fori(0, NT) as it:
                sp.wait_ge(S["x_loaded"], it * 16 + 16)
                sp.dma_start(qx[bass.ts(it, P), C:2 * C], x_in).then_inc(S["x_out"], 16)
                for j in range(2, SPI):
                    load_chunks(it * SPI + j, j % 2)
                with sp.If(it < NT - 1):
                    nxt = nc.s_assert_within(it + 1, 1, NT - 1, skip_runtime_bounds_check_because="the If has it < NT - 1")
                    nxt = sp.snap(nxt)
                    sp.wait_ge(S["z1_ready"], it + 1)
                    sp.wait_ge(S["x_out"], it * 16 + 16)
                    sp.dma_start(x_in, x[bass.ts(nxt, P), :]).then_inc(S["x_loaded"], 16)
                    for b in range(2):
                        load_chunks(nxt * SPI + b, b)
                sp.wait_ge(S["qkv_sb"], it * 3 + 3)
                sp.sem_inc(S["sp_held"], 1)
                sp.dma_start(qx[bass.ts(it, P), 0:C], qx_row[:, 0:C]).then_inc(S["qkv_out"], 16)
                sp.dma_start(kv[bass.ts(it, P), :], kv_row).then_inc(S["qkv_out"], 16)
            sp.wait_ge(S["x_out"], 16 * NT)
            sp.wait_ge(S["phase1_pe"], 1)
            sp.wait_ge(S["phase1_dve"], 1)
            sp.dma_start(Wo_sb, Wo.rearrange("(k p) n -> p k n", p=P)).then_inc(S["weights2"], 16)
            sp.dma_start(W1_sb, W1.rearrange("(k p) n -> p k n", p=P)).then_inc(S["weights2"], 16)
            sp.dma_start(W2_sb, W2.rearrange("(k p) n -> p k n", p=P)).then_inc(S["weights2"], 16)
            sp.wait_ge(S["ranked"], 16 * RPP)
            sp.dma_start(ranked_sb[:, :, :], rows_ranked.rearrange("(t p) w -> t p w", p=P)).then_inc(S["ranked_loaded"], 16)
            with nc.allow_non_contiguous_dma(reason="one word a row"):
                sp.dma_start(perm[:, 2:], rows_ranked[:, 0:1].rearrange("(t p) w -> p (t w)", p=P)).then_inc(S["ranked_loaded"], 16)
                sp.wait_ge(S["ng_ready"], 1)
                sp.dma_start(n_groups.rearrange("a t -> t a"), ng_i[:, :]).then_inc(S["ng_out"], 16)
            with sp.Fori(0, NT) as t:
                sp.wait_ge(S["row_used"], t)
                sp.dma_start(row_next[:, :], rows_ranked[bass.ts(t, P), :]).then_inc(S["row_loaded"], 16)

        @block.gpsimd
        def _(pool):
            def hold(semaphore, value):
                pool.wait_ge(semaphore, value)
                pool.sem_inc(S["pool_held"], 1)

            pool.iota(iota_i[:, :], pattern=[[1, P]], base=0, channel_multiplier=0).then_inc(S["consts_a"], 1)
            pool.iota(part_i[:, :], pattern=[[0, 1]], base=0, channel_multiplier=1).then_inc(S["consts_a"], 1)
            pool.iota(rid_i[:, :], pattern=[[1, LO]], base=0, channel_multiplier=LO).then_inc(S["consts_a"], 1)
            pool.memset(pad_rec[:, :, 0:HEADS], PAD_BIAS).then_inc(S["pad_ready"], 1)
            pool.memset(pad_rec[:, :, HEADS:HEADS + 1].bitcast(I32), NO_COL).then_inc(S["pad_ready"], 1)
            pool.memset(pad_rec[:, :, HEADS + 1:REC], 0.0).then_inc(S["pad_ready"], 1)
            pool.memset(rec_w[0][:, :, HEADS + 1:REC], 0.0).then_inc(S["consts_c"], 1)
            pool.memset(rec_w[1][:, :, HEADS + 1:REC], 0.0).then_inc(S["consts_c"], 1)
            pool.memset(region_a[:, COLS * (HEADS + 6) + C:], 0.0).then_inc(S["consts_c"], 1)
            pool.wait_ge(S["consts_c"], 3)
            pool.wait_ge(S["table_cleared"], 16 * (NBLK * GROUP // (P * PADN)))
            with pool.Fori(0, NT) as it:
                for j in range(SPI):
                    hold(S["pos_ready"], it * SPI + j + 1)
                    hold(S["rec_ready"], it * SPI + j + 1)
                    for s in range(STREAMS):
                        pool.indirect_dma_start(records, bass.IndirectOffsetOnAxis(ap=pos_i[j % 2][:, s:s + 1], axis=0),
                                                rec_w[j % 2][:, s, :], None).then_inc(SCAT[j % 2], 16)
            pool.wait_ge(S["rank_ready"], 1)
            for j in range(RPP):
                pool.indirect_dma_start(rows_ranked, bass.IndirectOffsetOnAxis(ap=rank_i[:, j:j + 1], axis=0),
                                        info_sb[:, j, :], None).then_inc(S["ranked"], 16)
            for h in range(2):
                pool.wait_ge(SCAT[h], 16 * STREAMS * STEPS // 2)
            pool.wait_ge(S["qkv_out"], 32 * NT)
            pool.wait_ge(S["x_out"], 16 * NT)
            pool.wait_ge(S["phase1_dve"], 1)
            pool.wait_ge(S["phase1_act"], 1)
            pool.wait_ge(S["ng_out"], 16)
            groups = pool.alloc_register("pool_groups")
            n_rec = pool.alloc_register("pool_recs")
            n_idx = pool.alloc_register("pool_idx")
            n_out = pool.alloc_register("pool_outs")
            since = pool.alloc_register("pool_since")
            n_resets = pool.alloc_register("pool_resets")
            n_tiles = pool.alloc_register("pool_tiles")
            n_x = pool.alloc_register("pool_x")
            for r in (n_tiles, n_x, groups, n_rec, n_idx, n_out, since, n_resets):
                pool.reg_mov(r, 0)

            def load_records(h):
                pool.reg_add(n_rec, n_rec, 1)
                pool.indirect_dma_start(rec[h][:, :, :].rearrange("p s r -> p (s r)"), None, blocks,
                                        bass.IndirectOffsetOnAxis(ap=idx[h][:, 0:1], axis=0)).then_inc(S["rec_loaded"], 16)

            def add_biases():
                hold(S["qx_loaded"], pool.snap(n_tiles) * 16)
                hold(S["s_ready"], pool.snap(n_x))
                pool.reg_add(n_x, n_x, 1)
                pool.tensor_tensor(x_bo, row_qx[:, C:2 * C], bo_all[:, :], ALU.add)
                pool.tensor_tensor(x_b2, row_qx[:, C:2 * C], b2_all[:, :], ALU.add).then_inc(S["x_ready"], 1)

            def send():
                with pool.If(pool.snap(n_tiles) > 2):
                    hold(S["out_ready"], pool.snap(n_out) + 1)
                    pool.reg_add(n_out, n_out, 1)
                    pool.indirect_dma_start(out, bass.IndirectOffsetOnAxis(ap=out_idx[:, 0:1], axis=0),
                                            out_w, None).then_inc(S["out_sent"], 16)

            def gather(h):
                g = pool.snap(groups)
                k = pool.snap(n_idx)
                hold(S["rec_loaded"], pool.snap(n_rec) * 16)
                hold(S["summed"], g * PAIRS + 1)
                pool.tensor_copy(bias_w[h][:, :, :], rec[h][:, :, 0:HEADS])
                pool.tensor_copy(cols[h][:, :].bitcast(I32), rec[h][:, :, HEADS].bitcast(I32))
                pool.tensor_scalar(idx[1 - h][:, :], idx[h][:, :], 1.0, row_w[:, 2:3], ALU.add, ALU.min).then_inc(S["idx_set"], 1)
                pool.reg_add(n_idx, n_idx, 1)
                hold(S["idx_set"], k + 1)
                load_records(1 - h)
                for s in range(GROUP):
                    if s % 2 == 0 and s > 0:
                        hold(S["summed"], g * PAIRS + s // 2 + 1)
                    pool.indirect_dma_start(KV[h][:, s, :], None, kv,
                                            bass.IndirectOffsetOnAxis(ap=cols[h][:, s:s + 1].bitcast(I32), axis=0),
                                            bounds_check=L - 1, oob_is_err=False).then_inc(KVS[h][s // 2], 16)
                pool.reg_add(groups, groups, 1)
                if h == 0:
                    pool.reg_add(since, since, 1)

            def reset():
                with pool.If(pool.snap(since) > RESET_AT):
                    pool.reg_add(n_resets, n_resets, 1)
                    hold(S["rec_loaded"], pool.snap(n_rec) * 16)
                    hold(S["quiet"], pool.snap(n_resets))
                    pool.drain()
                    pool.dma_reset(range(DMA_COUNTS[0].num, DMA_COUNTS[-1].num + 1))
                    pool.sem_clear(range(DMA_COUNTS[0].num, DMA_COUNTS[-1].num + 1))
                    pool.reg_mov(n_rec, 0)
                    pool.reg_mov(since, 0)
                    pool.drain().then_inc(S["restarted"], 1)

            count = pool.alloc_register("pool_count")
            pool.reg_mov(count, load_count(pool, 0))
            with pool.Fori(0, NT) as t:
                n = pool.snap(count, min_val=1, max_val=NBLK)
                pool.reg_add(n_tiles, n_tiles, 1)
                hold(S["row_loaded"], t * 16 + 16)
                pool.tensor_copy(row_w[:, :].bitcast(I32), row_next[:, :].bitcast(I32)).then_inc(S["row_used"], 1)
                hold(S["row_used"], t + 1)
                hold(S["x_ready"], t)
                hold(S["q_taken"], t)
                pool.indirect_dma_start(row_qx, None, qx,
                                        bass.IndirectOffsetOnAxis(ap=row_w[:, 0:1].bitcast(I32), axis=0)).then_inc(S["qx_loaded"], 16)
                def first_records(f):
                    k = pool.snap(n_idx)
                    hold(S["rec_loaded"], pool.snap(n_rec) * 16)
                    pool.tensor_copy(idx[f][:, :], row_w[:, 1:2].bitcast(I32)).then_inc(S["idx_set"], 1)
                    pool.reg_add(n_idx, n_idx, 1)
                    hold(S["idx_set"], k + 1)
                    load_records(f)

                def alone(stage):
                    if stage == 1:
                        next_count(pool, t, count)
                    if stage == PEEL - 2:
                        send()
                    if stage == PEEL - 1:
                        add_biases()

                def body(h, stage):
                    gather(h)
                    alone(stage)

                def tile(f):
                    first_records(f)
                    tile_groups(pool, n, f, body, alone, reset)

                by_half(pool, groups, tile)
                hold(S["qx_loaded"], t * 16 + 16)
                hold(S["idx_set"], pool.snap(n_idx))
            for i in range(max(NT - 2, 0), NT):
                pool.wait_ge(S["out_ready"], i + 1)
                pool.indirect_dma_start(out, bass.IndirectOffsetOnAxis(ap=out_idx[:, 0:1], axis=0),
                                        out_w, None).then_inc(S["out_sent"], 16)
            hold(S["rec_loaded"], pool.snap(n_rec) * 16)
            pool.wait_ge(S["out_sent"], 16 * NT)

        @block.scalar
        def _(act):
            for i, to in enumerate((qx_row, kv_row)):
                for b0 in range(0, TB, 4):
                    w = min(4, TB - b0) * P
                    act.wait_ge(S["turned"], i * ((TB + 3) // 4) + b0 // 4 + 1)
                    last = act.copy(to[:, b0 * P:b0 * P + w], bank[2 * i + b0 // 4][:, 0:w])
                last.then_inc(S["turned_sb"], 1)
            act.wait_ge(S["consts_c"], 2)
            act.wait_ge(S["edges_loaded"], 32)
            act.wait_ge(S["weights_loaded"], 16 * 13)
            act.wait_ge(S["info_ready"], 1)

            with act.Fori(0, NT) as it:
                def table(j):
                    st = it * SPI + j
                    act.wait_ge(S["counted1"], st + 1)
                    act.wait_ge(S["g_done"], st)
                    act.copy(table_sb, count_ps).then_inc(S["table_ready"], 1)

                def fill(j):
                    st = it * SPI + j
                    act.wait_ge(SCAT[j % 2], (it * (SPI // 2) + j // 2) * 16 * STREAMS)
                    act.copy(rec_w[j % 2][:, :, 0:HEADS],
                             edge_sb[:, bass.ds(st * (STREAMS * HEADS), STREAMS * HEADS)].rearrange("p (s h) -> p s h", s=STREAMS)
                             )
                    act.copy(rec_w[j % 2][:, :, HEADS:HEADS + 1].rearrange("p s o -> p (s o)").bitcast(I32),
                             dst_i[:, bass.ds(st * STREAMS, STREAMS)]).then_inc(S["rec_ready"], 1)

                act.wait_ge(S["stats1"], it + 1)
                act.activation(std[:, :], mv[:, 1:2], ACT.Sqrt, bias=eps_t[:, :]).then_inc(S["std1"], 1)
                table(0)
                fill(0)
                act.wait_ge(S["z1_turned"], it + 1)
                for c in range(KT):
                    last = act.activation(zT1[:, c * P:(c + 1) * P], turn_ps[:, c * P:(c + 1) * P], ACT.Identity,
                                          bias=ln1_cols[:, 1, c:c + 1], scale=ln1_cols[:, 0, c:c + 1])
                last.then_inc(S["z1_sb"], 1)
                for j in range(1, SPI):
                    table(j)
                    fill(j)
                act.wait_ge(S["qkv_out"], it * 32)
                for w, to in enumerate((qx_row[:, 0:C], kv_row[:, 0:C], kv_row[:, C:2 * C])):
                    act.wait_ge(S["qkv_done"], it * 3 + w + 1)
                    act.activation(to, qkv_ps[w][:, :], ACT.Copy, scale=SCALE if w == 0 else 1.0).then_inc(S["qkv_sb"], 1)
            act.drain()
            act.mul(b1_half[:, :], b1_col[:, :], 0.5).then_inc(S["phase1_act"], 1)
            act.drain()
            act.wait_ge(S["ng_out"], 16)
            groups = act.alloc_register("act_groups")
            n_scT = act.alloc_register("act_scT")
            n_vT = act.alloc_register("act_vT")
            n_end = act.alloc_register("act_end")
            for r in (groups, n_scT, n_vT, n_end):
                act.reg_mov(r, 0)

            def take_scT():
                n = act.snap(n_scT)
                act.wait_ge(S["scT_ready"], n + 1)
                act.copy(scT_sb, scT_ps).then_inc(S["scT_sb_ready"], 1)
                act.reg_add(n_scT, n_scT, 1)

            def take_vT():
                n = act.snap(n_vT)
                act.wait_ge(S["summed"], n * PAIRS + 3 * PAIRS)
                act.wait_ge(S["acc_ready"], n)
                act.copy(vT_sb, vT_ps[:, :]).then_inc(S["vT_sb_ready"], 1)
                act.reg_add(n_vT, n_vT, 1)

            def turn_att(k):
                act.wait_ge(S["att_turned"], k)
                act.copy(attT, turn_ps[:, :]).then_inc(S["att_sb"], 1)

            def std_of(stats_sem, std_sem, k):
                act.wait_ge(stats_sem, k)
                act.activation(std[:, :], mv[:, 1:2], ACT.Sqrt, bias=eps_t[:, :]).then_inc(std_sem, 1)

            def turn_z2(k):
                act.wait_ge(S["z2_turned"], k)
                for c in range(KT):
                    last = act.activation(z2T[:, c * P:(c + 1) * P], turn_ps[:, c * P:(c + 1) * P], ACT.Identity,
                                          bias=ln2_cols[:, 1, c:c + 1], scale=ln2_cols[:, 0, c:c + 1])
                last.then_inc(S["z2_sb"], 1)

            def hidden(k, a):
                act.wait_ge(H_DONE[a], k)
                for c in range(a * HT // 2, (a + 1) * HT // 2):
                    ps = h_ps[c // 4][:, (c % 4) * P:(c % 4 + 1) * P]
                    act.activation(th[:, c * P:(c + 1) * P], ps, ACT.Tanh, bias=b1_half[:, c:c + 1], scale=0.5)
                    last = act.activation(hb[:, c * P:(c + 1) * P], ps, ACT.Identity, bias=b1_half[:, c:c + 1], scale=0.5)
                last.then_inc(H_ACT[a], 1)

            count = act.alloc_register("act_count")
            act.reg_mov(count, load_count(act, 0))
            with act.Fori(0, NT) as t:
                n = act.snap(count, min_val=1, max_val=NBLK)

                def norms(stage):
                    if stage == 1:
                        with act.If(t > 1):
                            act.reg_add(n_end, n_end, 1)
                            std_of(S["stats_end"], S["std_end"], act.snap(n_end))
                    if stage == 2:
                        with act.If(t > 0):
                            std_of(S["stats_mid"], S["std_mid"], t)

                def tail(stage):
                    if stage == 0:
                        with act.If(t > 0):
                            turn_att(t)
                    if stage == 2:
                        with act.If(t > 0):
                            turn_z2(t)
                def middle(stage):
                    if stage == 1:
                        next_count(act, t, count)
                    if stage == 3:
                        with act.If(t > 0):
                            hidden(t, 0)
                    if stage == 4:
                        with act.If(t > 0):
                            hidden(t, 1)

                def alone(stage):
                    norms(stage)
                    middle(stage)
                    tail(stage)

                def body(h, stage):
                    g = act.snap(groups)
                    take_scT()
                    norms(stage)
                    act.wait_ge(S["sc_ready"], g + 1)
                    act.activation(pr[h][:, :, :], sc[h][:, :, :], ACT.Exp).then_inc(S["p_ready"], 1)
                    if stage == 0:
                        with act.If(t > 0):
                            take_vT()
                    else:
                        take_vT()
                    act.drain()
                    for s in range(SUB, GROUP):
                        for hd in range(HEADS):
                            v = KV[h][:, s, C + hd * D:C + (hd + 1) * D]
                            last = act.activation(v, v, ACT.Copy, scale=pr[h][:, s, hd:hd + 1])
                        if s % 2:
                            last.then_inc(S["v_act"], 1)
                        if s == GROUP - 3:
                            middle(stage)
                    act.reg_add(groups, groups, 1)
                    tail(stage)

                by_half(act, groups, lambda f: tile_groups(act, n, f, body, alone))
            std_of(S["stats_end"], S["std_end"], NT - 1)
            take_vT()
            turn_att(NT)
            std_of(S["stats_mid"], S["std_mid"], NT)
            turn_z2(NT)
            for a in range(2):
                hidden(NT, a)
            std_of(S["stats_end"], S["std_end"], NT)

        @block.vector
        def _(dve):
            def hold(semaphore, value):
                dve.wait_ge(semaphore, value)
                dve.sem_inc(S["dve_held"], 1)

            dve.wait_ge(S["consts_a"], 3)
            dve.tensor_copy(iota_f[:, :], iota_i[:, :])
            dve.tensor_copy(part_f[:, :], part_i[:, :])
            dve.tensor_copy(rid_f[:, :], rid_i[:, :])
            dve.memset(zeros_bf[:, :], 0.0)
            dve.memset(ones[:, :], 1.0)
            dve.memset(ones_lo[:, :], 1.0)
            dve.memset(eps_t[:, :], EPS)
            dve.drain()
            dve.tensor_scalar(quarter_i[:, :], part_i[:, :], FOLD.bit_length() - 1, None, ALU.arith_shift_right)
            dve.drain()
            dve.tensor_copy(quarter_f[:, :], quarter_i[:, :])
            dve.drain()
            dve.tensor_scalar(fold[:, :], iota_f[:, 0:SH], quarter_f[:, 0:1], None, ALU.is_equal)
            dve.tensor_scalar(ident[:, :], iota_f[:, :], part_f[:, 0:1], None, ALU.is_equal)
            dve.tensor_scalar(tri[:, :], iota_f[:, :], part_f[:, 0:1], None, ALU.is_lt)
            dve.tensor_scalar(triT[:, :], iota_f[:, :], part_f[:, 0:1], None, ALU.is_gt)
            dve.wait_ge(S["src_loaded"], 16)
            dve.tensor_copy(src_f, int_a)
            dve.tensor_scalar(int_b, int_a, LO.bit_length() - 1, None, ALU.arith_shift_right)
            dve.drain()
            dve.tensor_copy(hi_f, int_b)
            dve.drain()
            dve.tensor_scalar(int_b, int_a, LO - 1, None, ALU.bitwise_and)
            dve.drain()
            dve.tensor_copy(lo_f, int_b)
            dve.drain()
            dve.drain().then_inc(S["keys_ready"], 1)

            def one_hots(b, c0):
                dve.tensor_tensor(hi_oh[b][:, :, :], hi_f[:, bass.ds(c0, STREAMS)].unsqueeze(2).broadcast_to([P, STREAMS, HI]),
                                  iota_f[:, 0:HI].unsqueeze(1).broadcast_to([P, STREAMS, HI]), ALU.is_equal)
                return dve.tensor_tensor(lo_oh[b][:, :, :], lo_f[:, bass.ds(c0, STREAMS)].unsqueeze(2).broadcast_to([P, STREAMS, LO]),
                                         iota_f[:, 0:LO].unsqueeze(1).broadcast_to([P, STREAMS, LO]), ALU.is_equal)

            with dve.Fori(0, STEPS // 2) as i:
                for b in range(2):
                    dve.wait_ge(S["onehots_free"], i * 2 + b + 1)
                    one_hots(b, (i * 2 + b) * STREAMS).then_inc(S["onehots_ready"], 1)

            dve.wait_ge(S["hist_done"], 1)
            dve.tensor_copy(hist[:, :, :].rearrange("h s l -> h (s l)"), count_ps)
            dve.drain()
            dve.tensor_reduce(deg[:, :], hist[:, :, :].rearrange("h s l -> h l s"), AX.X, ALU.add)
            dve.drain()
            dve.tensor_scalar(deg_i[:, :], deg[:, :], float(GROUP - 1), None, ALU.add)
            dve.drain()
            dve.tensor_scalar(nb_i[:, :], deg_i[:, :], GROUP.bit_length() - 1, None, ALU.arith_shift_right)
            dve.drain()
            dve.tensor_scalar(width[:, :], nb_i[:, :], 1.0, None, ALU.add)
            dve.drain()
            dve.tensor_tensor_scan(cum[:, :], ones_lo[:, :], width[:, :], 0.0, ALU.mult, ALU.add)
            dve.drain()
            dve.tensor_copy(offs[:, :], cum[:, LO - 1:LO]).then_inc(S["prefix_in"], 1)
            dve.tensor_tensor(blk[:, :], cum[:, :], width[:, :], ALU.subtract)
            dve.drain()
            dve.wait_ge(S["prefix_out"], 1)
            dve.tensor_scalar(blk[:, :], blk[:, :], turn_ps[0:HI, 0:1], None, ALU.add)
            dve.drain()
            dve.tensor_scalar(start_tab[:, 0, :], blk[:, :], float(GROUP), None, ALU.mult)
            dve.drain()
            for s in range(1, STREAMS):
                dve.tensor_tensor(start_tab[:, s, :], start_tab[:, s - 1, :], hist[:, s - 1, :], ALU.add)
                dve.drain()
            dve.tensor_copy(info_w[:, :, 0].bitcast(I32), rid_i[:, :])
            dve.tensor_copy(info_w[:, :, 1].bitcast(I32), blk[:, :])
            dve.tensor_tensor(info_w[:, :, 2], blk[:, :], nb_i[:, :], ALU.add)
            dve.tensor_copy(info_w[:, :, 3], nb_i[:, :])
            dve.tensor_scalar(key_w[:, :], nb_i[:, :], 2047.0, float(L), ALU.min, ALU.mult)
            dve.drain()
            dve.tensor_tensor(key_w[:, :], key_w[:, :], rid_f[:, :], ALU.subtract)
            dve.drain().then_inc(S["info_ready"], 1)

            dve.wait_ge(S["keys_loaded"], 48)
            def hits(b, n):
                dve.wait_ge(SRCB[b], n * 32)
                dve.tensor_scalar(hitT[b], hib[b], part_f[0:HI, 0:1], None, ALU.is_equal).then_inc(S["hit_ready"], 1)

            hits(0, 1)
            with dve.Fori(0, NT) as it:
                def step(j):
                    st = it * SPI + j
                    b = j % 2
                    dve.wait_ge(S["counted1"], st)
                    one_hots(b, st * STREAMS).then_inc(S["oh1_ready"], 1)
                    if j < SPI - 1:
                        hits(1 - b, it * (SPI // 2) + (j + 1) // 2 + 1)
                    else:
                        with dve.If(it < NT - 1):
                            hits(0, (it + 1) * (SPI // 2) + 1)
                    dve.drain()
                    for s in range(STREAMS):
                        last = dve.scalar_tensor_tensor(eq[:, s * P:(s + 1) * P], srcb[b][:, s * P:(s + 1) * P],
                                                        src_f[:, bass.ds(st * STREAMS + s, 1)], tri[:, :],
                                                        ALU.is_equal, ALU.mult, accum_out=rank_w[:, s:s + 1])
                    last.then_inc(S["srcb_used"], 1)
                    dve.wait_ge(S["g_done"], st + 1)
                    dve.tensor_tensor(sel, sel_ps[b][:, :], lo_oh[b][:, :, :].rearrange("p s l -> p (s l)"), ALU.mult).then_inc(S["sel_free"], 1)
                    dve.drain()
                    dve.tensor_reduce(base_w[:, :], sel.rearrange("p (s l) -> p s l", s=STREAMS), AX.X, ALU.add)
                    dve.drain()
                    dve.wait_ge(SCAT[b], (it * (SPI // 2) + j // 2) * 16 * STREAMS)
                    dve.tensor_tensor(pos_i[b][:, :], base_w[:, :], rank_w[:, :], ALU.add).then_inc(S["pos_ready"], 1)

                dve.wait_ge(S["x_loaded"], it * 16 + 16)
                dve.bn_stats(stats[:, :], x_in)
                dve.drain()
                dve.bn_aggr(mv[:, :], stats[:, :]).then_inc(S["stats1"], 1)
                step(0)
                dve.wait_ge(S["std1"], it + 1)
                dve.reciprocal(rstd[:, :], std[:, :])
                dve.drain()
                dve.wait_ge(S["z1_turned"], it)
                dve.tensor_scalar(z1, x_in, mv[:, 0:1], rstd[:, 0:1], ALU.subtract, ALU.mult).then_inc(S["z1_ready"], 1)
                step(1)
                dve.tensor_scalar(greater, keys_all, key_col[:, bass.ds(it, 1)], 0.0, ALU.is_gt, ALU.add,
                                  accum_out=rank_f[:, bass.ds(it, 1)])
                for j in range(2, SPI):
                    step(j)
            dve.drain()
            dve.tensor_copy(rank_i[:, :], rank_f[:, :]).then_inc(S["rank_ready"], 1)
            dve.drain().then_inc(S["phase1_dve"], 1)
            dve.wait_ge(S["ranked_loaded"], 32)
            dve.tensor_reduce(ng_f[:, :], ranked_sb[:, :, 3], AX.X, ALU.max)
            dve.drain()
            dve.tensor_scalar(ng_i[:, :], ng_f[:, :], 1.0, None, ALU.max).then_inc(S["ng_ready"], 1)
            dve.wait_ge(S["ng_out"], 16)
            dve.wait_ge(S["qkv_out"], 32 * NT)
            groups = dve.alloc_register("dve_groups")
            n_prods = dve.alloc_register("dve_prods")
            n_acc = dve.alloc_register("dve_acc")
            loads = [dve.alloc_register(f"dve_loads{h}") for h in range(2)]
            n_out = dve.alloc_register("dve_outs")
            n_resets = dve.alloc_register("dve_resets")
            for r in (groups, n_prods, n_acc, *loads, n_out, n_resets):
                dve.reg_mov(r, 0)

            def reset():
                with dve.If(dve.snap(loads[0]) > RESET_AT):
                    dve.reg_add(n_resets, n_resets, 1)
                    dve.drain().then_inc(S["quiet"], 1)
                    hold(S["restarted"], dve.snap(n_resets))
                    for r in loads:
                        dve.reg_mov(r, 0)

            def heads(ap):
                return ap.rearrange("p (h d) -> p h d", h=HEADS)

            def products(h):
                n = dve.snap(n_prods)
                loaded = dve.snap(loads[h]) * (16 * 2) + 16 * 2
                dve.wait_ge(S["scT_ready"], n)
                for pair in range(PAIRS):
                    of = slice(2 * pair, 2 * pair + 2)
                    dve.wait_ge(KVS[h][pair], loaded)
                    dve.tensor_tensor(prods[:, of, :], KV[h][:, of, 0:C],
                                      q_w.unsqueeze(1).broadcast_to([P, 2, C]), ALU.mult).then_inc(S["prods_ready"], 1)
                dve.reg_add(n_prods, n_prods, 1)
                dve.reg_add(loads[h], loads[h], 1)

            def add_sum():
                n = dve.snap(n_acc)
                dve.wait_ge(S["acc_ready"], n + 1)
                dve.tensor_tensor(acc, acc, acc_ps[:, :], ALU.add).then_inc(S["acc_taken"], 1)
                dve.reg_add(n_acc, n_acc, 1)

            def add_weights(h):
                dve.tensor_reduce(l_sum[:, :], pr[h][:, 0:GROUP, :].rearrange("p s h -> p h s"), AX.X, ALU.add)
                dve.tensor_tensor(l_run[:, :], l_run[:, :], pr[h][:, GROUP, :], ALU.mult)
                dve.drain()
                dve.tensor_tensor(l_run[:, :], l_run[:, :], l_sum[:, :], ALU.add)

            def scale_acc(h):
                dve.tensor_tensor(heads(acc), heads(acc), pr[h][:, GROUP, :].unsqueeze(2).broadcast_to([P, HEADS, D]), ALU.mult)
                dve.drain()

            def statistics(ps, stats_sem):
                dve.bn_stats(stats[:, :], ps)
                dve.drain()
                dve.bn_aggr(mv[:, :], stats[:, :]).then_inc(stats_sem, 1)

            def residual_stats(k):
                dve.wait_ge(S["x_ready"], k)
                dve.wait_ge(S["wo_done"], k)
                dve.tensor_tensor(z2, wo_ps[:, :], x_bo, ALU.add)
                dve.drain()
                statistics(z2, S["stats_mid"])

            def residual(k):
                dve.tensor_tensor(s_w, z2, x_b2, ALU.add).then_inc(S["s_ready"], 1)
                dve.wait_ge(S["std_mid"], k)
                dve.reciprocal(rstd[:, :], std[:, :])
                dve.drain()
                dve.tensor_scalar(z2, z2, mv[:, 0:1], rstd[:, 0:1], ALU.subtract, ALU.mult).then_inc(S["z2_ready"], 1)

            def silu(k, a):
                of = slice(a * HID // 2, (a + 1) * HID // 2)
                dve.wait_ge(H_ACT[a], k)
                dve.scalar_tensor_tensor(hT[:, of], th[:, of], 1.0, hb[:, of], ALU.add, ALU.mult).then_inc(H_READY[a], 1)

            def last_stats():
                dve.wait_ge(S["y_done"], dve.snap(n_out) + 1)
                dve.tensor_tensor(s_w, s_w, y_ps[:, :], ALU.add).then_inc(S["y_taken"], 1)
                dve.drain()
                statistics(s_w, S["stats_end"])

            def last_norm(column):
                dve.wait_ge(S["std_end"], dve.snap(n_out) + 1)
                dve.reciprocal(rstd[:, :], std[:, :])
                dve.drain()
                hold(S["out_sent"], dve.snap(n_out) * 16)
                dve.reg_add(n_out, n_out, 1)
                dve.tensor_copy(out_idx[:, :], perm[:, column].bitcast(I32))
                dve.tensor_scalar(out_w, s_w, mv[:, 0:1], rstd[:, 0:1], ALU.subtract, ALU.mult)
                dve.drain().then_inc(S["out_ready"], 1)

            def finish():
                add_sum()
                dve.drain()
                dve.tensor_scalar(l_inv[:, :], l_run[:, :], TINY, None, ALU.max)
                dve.drain()
                dve.reciprocal(l_inv[:, :], l_inv[:, :])
                dve.drain()
                dve.tensor_tensor(heads(att), heads(acc), l_inv[:, :].unsqueeze(2).broadcast_to([P, HEADS, D]), ALU.mult).then_inc(S["att_ready"], 1)

            count = dve.alloc_register("dve_count")
            dve.reg_mov(count, load_count(dve, 0))
            with dve.Fori(0, NT) as t:
                n = dve.snap(count, min_val=1, max_val=NBLK)
                dve.drain()
                hold(S["qx_loaded"], t * 16 + 16)
                dve.tensor_copy(q_w, row_qx[:, 0:C]).then_inc(S["q_taken"], 1)
                dve.drain()

                def gap(stage):
                    if stage == 3:
                        next_count(dve, t, count)
                    if stage == 0:
                        with dve.If(t > 1):
                            silu(dve.snap(n_out) + 1, 1)
                    if stage == 1:
                        with dve.If(t > 1):
                            last_stats()
                    if stage == 2:
                        with dve.If(t > 0):
                            residual_stats(t)
                    if stage == 4:
                        with dve.If(t > 0):
                            silu(t, 0)

                def late(stage):
                    if stage == 1:
                        with dve.If(t > 1):
                            last_norm(bass.ds(t, 1))

                def tail(stage):
                    if stage == 2:
                        with dve.If(t > 0):
                            residual(t)

                def alone(stage):
                    gap(stage)
                    late(stage)
                    tail(stage)

                def body(h, stage):
                    g = dve.snap(groups)
                    products(h)
                    if stage > 1:
                        add_sum()
                    if stage > 0:
                        dve.drain()
                        add_weights(1 - h)
                    gap(stage)
                    if stage == 0:
                        dve.memset(m_run[:, :], FLOOR)
                    s_all = sc[h][:, 0:GROUP, :]
                    dve.wait_ge(S["sc_summed"], g + 1)
                    dve.tensor_tensor(s_all, sc_ps.rearrange("p (s h) -> p s h", s=GROUP), bias_w[h][:, :, :], ALU.add)
                    dve.drain()
                    dve.tensor_reduce(m_new[:, :], s_all.rearrange("p s h -> p h s"), AX.X, ALU.max)
                    dve.drain()
                    dve.tensor_tensor(m_new[:, :], m_new[:, :], m_run[:, :], ALU.max)
                    dve.drain()
                    dve.tensor_tensor(s_all, s_all, m_new[:, :].unsqueeze(1).broadcast_to([P, GROUP, HEADS]), ALU.subtract)
                    dve.tensor_tensor(sc[h][:, GROUP, :], m_run[:, :], m_new[:, :], ALU.subtract).then_inc(S["sc_ready"], 1)
                    dve.drain()
                    dve.tensor_copy(m_run[:, :], m_new[:, :])
                    if stage > 0:
                        scale_acc(1 - h)
                    late(stage)
                    dve.wait_ge(S["p_ready"], g + 1)
                    for s0 in range(0, SUB, 2):
                        v = KV[h][:, s0:s0 + 2, C:2 * C].rearrange("p s (h d) -> p s h d", h=HEADS)
                        dve.tensor_tensor(v, v, pr[h][:, s0:s0 + 2, :].unsqueeze(3).broadcast_to([P, 2, HEADS, D]),
                                          ALU.mult).then_inc(S["v_dve"], 1)
                    tail(stage)
                    if stage == 0:
                        with dve.If(t > 0):
                            finish()
                        dve.drain()
                        dve.memset(l_run[:, :], 0.0)
                        dve.memset(acc, 0.0)
                    dve.reg_add(groups, groups, 1)

                by_half(dve, groups, lambda f: tile_groups(dve, n, f, body, alone, reset))
                with dve.If(n > 1):
                    add_sum()
                    dve.drain()

                def close(f):
                    add_weights(1 - f)
                    scale_acc(1 - f)

                dve.drain()
                by_half(dve, groups, close)
            silu(NT - 1, 1)
            last_stats()
            last_norm(slice(NT, NT + 1))
            finish()
            residual_stats(NT)
            residual(NT)
            silu(NT, 0)
            silu(NT, 1)
            last_stats()
            last_norm(slice(NT + 1, NT + 2))

        @block.tensor
        def _(pe):
            pe.wait_ge(S["keys_ready"], 1)
            for i, of in enumerate((src_f, hi_f)):
                for b in range(TB):
                    last = pe.transpose(bank[2 * i + b // 4][:, (b % 4) * P:(b % 4 + 1) * P], of[:, b * P:(b + 1) * P], ident[:, :])
                    if b % 4 == 3 or b == TB - 1:
                        last.then_inc(S["turned"], 1)
            pe.wait_ge(S["turned_sb"], 2)
            pe.matmul(count_ps, zeros_bf[:, 0:HI], zeros_bf[:, :], start=True, stop=True)
            pe.sem_inc(S["onehots_free"], 2)
            pe.sem_inc(S["srcb_used"], 2)

            def count(b):
                for s in range(STREAMS):
                    last = pe.matmul(count_ps[:, s * LO:(s + 1) * LO], hi_oh[b][:, s, :], lo_oh[b][:, s, :],
                                     start=False, stop=True, skip_group_check=True)
                return last

            with pe.Fori(0, STEPS // 2) as i:
                for b in range(2):
                    pe.wait_ge(S["onehots_ready"], i * 2 + b + 1)
                    count(b).then_inc(S["onehots_free"], 1)
            pe.wait_ge(S["onehots_free"], STEPS + 2)
            pe.sem_inc(S["hist_done"], 1)
            pe.wait_ge(S["prefix_in"], 1)
            pe.matmul(turn_ps[0:HI, 0:1], triT[0:HI, 0:HI], offs[:, :], start=True, stop=True).then_inc(S["prefix_out"], 1)
            pe.wait_ge(S["info_ready"], 1)
            pe.matmul(count_ps, ident[0:HI, 0:HI], start_tab[:, :, :].rearrange("h s l -> h (s l)"),
                      start=True, stop=True).then_inc(S["counted1"], 1)
            pe.wait_ge(S["weights_loaded"], 16 * 13)

            pe.sem_inc(S["sel_free"], 1)
            with pe.Fori(0, NT) as it:
                def step(j):
                    st = it * SPI + j
                    b = j % 2
                    pe.wait_ge(S["hit_ready"], st + 1)
                    pe.wait_ge(S["table_ready"], st + 1)
                    pe.wait_ge(S["sel_free"], st)
                    for s in range(STREAMS):
                        last = pe.matmul(sel_ps[b][:, s * LO:(s + 1) * LO], hitT[b][:, s * P:(s + 1) * P],
                                         table_sb[:, s * LO:(s + 1) * LO], start=True, stop=True)
                    last.then_inc(S["g_done"], 1)
                    pe.wait_ge(S["oh1_ready"], st + 1)
                    count(b).then_inc(S["counted1"], 1)

                def project(w):
                    pe.wait_ge(S["qkv_sb"], it * 3)
                    pe.matmul(qkv_ps[w][:, :], ones[:, :], bias3[:, w * C:(w + 1) * C], start=True, stop=False)
                    for c in range(KT):
                        last = pe.matmul(qkv_ps[w][:, :], zT1[:, c * P:(c + 1) * P], Wqkv[:, w, c, :],
                                         start=False, stop=c == KT - 1)
                    last.then_inc(S["qkv_done"], 1)

                step(0)
                pe.wait_ge(S["z1_ready"], it + 1)
                for c in range(KT):
                    last = pe.transpose(turn_ps[:, c * P:(c + 1) * P], z1[:, c * P:(c + 1) * P], ident[:, :])
                last.then_inc(S["z1_turned"], 1)
                for j in range(1, SPI):
                    step(j)
                    if j == 1:
                        pe.wait_ge(S["z1_sb"], it + 1)
                    project(j - 1)
                for w in range(SPI - 1, 3):
                    project(w)
            pe.wait_ge(S["qkv_done"], 3 * NT)
            pe.sem_inc(S["phase1_pe"], 1)
            pe.wait_ge(S["qkv_sb"], 3 * NT)
            pe.wait_ge(S["sel_free"], STEPS + 1)
            pe.wait_ge(S["weights2"], 48)
            pe.wait_ge(S["ng_out"], 16)
            groups = pe.alloc_register("pe_groups")
            n_scT = pe.alloc_register("pe_scT")
            n_acc = pe.alloc_register("pe_acc")
            n_down = pe.alloc_register("pe_down")
            for r in (groups, n_scT, n_acc, n_down):
                pe.reg_mov(r, 0)
            pe.sem_inc(S["summed"], 2 * PAIRS)
            pe.sem_inc(S["y_taken"], 1)
            prod_cols = prods.rearrange("p s (h j i) -> p i (s h) j", h=HEADS, j=FOLD)

            def sum_d(a):
                n = pe.snap(n_scT)
                pe.wait_ge(S["prods_ready"], n * PAIRS + (a + 1) * (PAIRS // 2))
                for i in range(D // FOLD):
                    last = pe.matmul(scT_ps[:, a * P:(a + 1) * P], prod_cols[:, i, a * SH:(a + 1) * SH], ident[:, :],
                                     start=i == 0, stop=i == D // FOLD - 1, is_transpose=True)
                if a == 1:
                    last.then_inc(S["scT_ready"], 1)

            def turn_scores():
                n = pe.snap(n_scT)
                pe.wait_ge(S["sc_ready"], n)
                pe.wait_ge(S["scT_sb_ready"], n + 1)
                for a in range(2):
                    last = pe.matmul(sc_ps[:, a * SH:(a + 1) * SH], scT_sb[:, a * P:(a + 1) * P], fold[:, :], start=True, stop=True)
                last.then_inc(S["sc_summed"], 1)
                pe.reg_add(n_scT, n_scT, 1)

            def turn_sum():
                n = pe.snap(n_acc)
                pe.wait_ge(S["vT_sb_ready"], n + 1)
                pe.wait_ge(S["acc_taken"], n)
                for c in range(KT):
                    last = pe.transpose(acc_ps[:, c * P:(c + 1) * P], vT_sb[:, c * P:(c + 1) * P], ident[:, :])
                last.then_inc(S["acc_ready"], 1)
                pe.reg_add(n_acc, n_acc, 1)

            def sum_v(h, pair):
                g = pe.snap(groups)
                if pair == 0:
                    pe.wait_ge(S["vT_sb_ready"], g)
                if pair < PAIRS // 2:
                    pe.wait_ge(S["v_dve"], g * (PAIRS // 2) + pair + 1)
                if pair >= PAIRS // 2:
                    pe.wait_ge(S["v_act"], g * (PAIRS // 2) + pair - PAIRS // 2 + 1)
                for s in (2 * pair, 2 * pair + 1):
                    for c in range(KT):
                        last = pe.matmul(vT_ps[:, c * P:(c + 1) * P], KV[h][:, s, C + c * P:C + (c + 1) * P], ident[:, :],
                                         start=s == 0 and c == 0, stop=s == GROUP - 1, is_transpose=True,
                                         skip_group_check=True)
                last.then_inc(S["summed"], 1)

            def last_pair(h):
                sum_v(h, PAIRS - 1)
                pe.reg_add(groups, groups, 1)

            def turn_att(k):
                pe.wait_ge(S["att_ready"], k)
                for c in range(KT):
                    last = pe.transpose(turn_ps[:, c * P:(c + 1) * P], att[:, c * P:(c + 1) * P], ident[:, :])
                last.then_inc(S["att_turned"], 1)

            def out_proj(k, a):
                if a == 0:
                    pe.wait_ge(S["y_taken"], k)
                    pe.wait_ge(S["att_sb"], k)
                for c in range(a * KT // 2, (a + 1) * KT // 2):
                    last = pe.matmul(wo_ps[:, :], attT[:, c * P:(c + 1) * P], Wo_sb[:, c, :], start=c == 0, stop=c == KT - 1)
                if a == 1:
                    last.then_inc(S["wo_done"], 1)

            def turn_z2(k):
                pe.wait_ge(S["z2_ready"], k)
                for c in range(KT):
                    last = pe.transpose(turn_ps[:, c * P:(c + 1) * P], z2[:, c * P:(c + 1) * P], ident[:, :])
                last.then_inc(S["z2_turned"], 1)

            def up(k, a):
                if a == 0:
                    pe.wait_ge(S["z2_sb"], k)
                for m in range(a * HT // 2, (a + 1) * HT // 2):
                    for c in range(KT):
                        last = pe.matmul(h_ps[m // 4][:, (m % 4) * P:(m % 4 + 1) * P], W1_sb[:, c, m * P:(m + 1) * P],
                                         z2T[:, c * P:(c + 1) * P], start=c == 0, stop=c == KT - 1)
                last.then_inc(H_DONE[a], 1)

            def down(k, a):
                pe.wait_ge(H_READY[a], k)
                if a == 0:
                    pe.wait_ge(S["s_ready"], k)
                for m in range(a * HT // 2, (a + 1) * HT // 2):
                    last = pe.matmul(y_ps[:, :], hT[:, m * P:(m + 1) * P], W2_sb[:, m, :], start=m == 0, stop=m == HT - 1)
                if a == 1:
                    last.then_inc(S["y_done"], 1)

            def behind(k, stage, a):
                if stage in (0, 2):
                    if a == 1:
                        (turn_att if stage == 0 else turn_z2)(k)
                elif stage < 4:
                    (out_proj if stage == 1 else up)(k, a)
                elif a == 0:
                    down(k, 0)

            count = pe.alloc_register("pe_count")
            pe.reg_mov(count, load_count(pe, 0))
            with pe.Fori(0, NT) as t:
                n = pe.snap(count, min_val=1, max_val=NBLK)

                def tail(stage, a):
                    if (stage, a) == (1, 1):
                        next_count(pe, t, count)
                    if (stage, a) == (0, 0):
                        with pe.If(t > 1):
                            pe.reg_add(n_down, n_down, 1)
                            down(pe.snap(n_down), 1)
                    if stage < PEEL and (stage not in (0, 2) or a == 1) and (stage, a) != (4, 1):
                        with pe.If(t > 0):
                            behind(t, stage, a)

                def alone(stage):
                    for a in range(2):
                        tail(stage, a)

                def body(h, stage):
                    if stage == 0:
                        with pe.If(t > 0):
                            sum_v(1 - h, PAIRS - 2)
                    else:
                        sum_v(1 - h, PAIRS - 2)
                    sum_d(0)
                    sum_d(1)
                    if stage == 0:
                        with pe.If(t > 0):
                            last_pair(1 - h)
                    else:
                        last_pair(1 - h)
                    turn_scores()
                    tail(stage, 0)
                    if stage == 0:
                        with pe.If(t > 0):
                            turn_sum()
                    else:
                        turn_sum()
                    for pair in range(PAIRS // 2):
                        sum_v(h, pair)
                    tail(stage, 1)

                by_half(pe, n_scT, lambda f: tile_groups(pe, n, f, body, alone))

            def rest(h):
                sum_v(h, PAIRS - 2)
                last_pair(h)

            by_half(pe, groups, rest)
            down(NT - 1, 1)
            turn_sum()
            for stage in range(PEEL):
                for a in range(2):
                    behind(NT, stage, a)
            down(NT, 1)


_INS = ["x", "src", "dst", "edge_attr_8"] + ["L0_gnn_" + n for n in (
    "Wq", "bq", "Wk", "bk", "Wv", "bv", "Wo", "bo", "ln1_g", "ln1_b", "ln2_g", "ln2_b", "W1", "b1", "W2", "b2")]


def kernel(**inputs):
    import numpy as _np
    import concourse.bacc as _bacc
    from concourse import mybir as _mybir
    from concourse.bass_utils import run_bass_kernel_spmd as _run

    nc = _bacc.Bacc("TRN2", target_bir_lowering=False, num_devices=1)
    arrays, args = {}, []
    for name in _INS:
        a = _np.ascontiguousarray(inputs[name])
        arrays[f"in_{name}_dram"] = a
        args.append(nc.dram_tensor(f"in_{name}_dram", a.shape, _mybir.dt.from_np(a.dtype), kind="ExternalInput").ap())
    shape = inputs["x"].shape
    args.append(nc.dram_tensor("out_0_dram", shape, _mybir.dt.float32, kind="ExternalOutput").ap())
    layer_kernel(nc, *args)
    r = _run(nc, [arrays], core_ids=[0])
    return r.results[0]["out_0_dram"]
```
